# Optimizing a Trainium2 kernel written in Bass

```python
import numpy as np
import jax
import jax.numpy as jnp

def _softmax(x, axis=-1):
    return jax.nn.softmax(x, axis=axis)
def _gelu(x):
    return jax.nn.gelu(x, approximate=True)
def _silu(x):
    return jax.nn.silu(x)
def _sigmoid(x):
    return jax.nn.sigmoid(x)
def _layernorm(x, axis=-1, eps=1e-5):
    m = jnp.mean(x, axis=axis, keepdims=True)
    v = jnp.var(x, axis=axis, keepdims=True)
    return (x - m) / jnp.sqrt(v + eps)
def _scatter_add(tgt, idx, src, axis=0):
    return tgt.at[idx].add(src)
def _segment_sum(src, seg, n):
    return jax.ops.segment_sum(src, seg, n)

kernel_name = 'mk_adj_seq_d1_adj_512_87d4fe'

def setup_inputs(seed: int = 0):
    np.random.seed(seed)
    _w = jnp.asarray
    def _rec_inputs():
        import jax
        import jax.numpy as jnp
        _gk = jax.random.key(seed)
        x = -0.0005207 + 1.001 * jax.random.normal(jax.random.fold_in(_gk, 1), (8192, 512), jnp.float32)
        _w = (1.0 + jnp.arange(8192, dtype=jnp.float32)) ** -0.5
        _w = _w / _w.mean()
        _pij = jnp.clip(0.000488281 * _w[:, None] * _w[None, :], 0.0, 1.0)
        _a = jax.random.uniform(jax.random.fold_in(_gk, 2), (8192, 8192)) < _pij
        adj = _a.astype(jnp.int32)
        return x, adj
    x, adj = _rec_inputs()
    def _L0_gnn_setup():
        import jax, jax.numpy as jnp
        import numpy as np
        N, DIM = (4096, 512)
        F_OUT = DIM // 8
        HID = int(DIM * 2.0)
        ALPHA = 0.2
        MASK_VAL = -9000000000000000.0

        def _layernorm(x, g, b, eps=1e-05):
            mu = x.mean(-1, keepdims=True)
            var = ((x - mu) ** 2).mean(-1, keepdims=True)
            return (x - mu) * jax.lax.rsqrt(var + eps) * g + b
        key = jax.random.key(seed)
        ks = jax.random.split(key, 8)
        x = jax.random.normal(ks[0], (N, DIM), jnp.float32)
        adj = jax.random.randint(ks[1], (N, N), 0, 2, jnp.int32)
        W = jax.random.normal(ks[2], (DIM, F_OUT), jnp.float32) * 0.1
        a = jax.random.normal(ks[3], (2 * F_OUT, 1), jnp.float32) * 0.1
        fc_w = jax.random.normal(ks[4], (DIM, F_OUT), jnp.float32) * 0.1
        fc_b = jnp.zeros((DIM,), jnp.float32)
        ln1_g = jnp.ones((DIM,), jnp.float32)
        ln1_b = jnp.zeros((DIM,), jnp.float32)
        ln2_g = jnp.ones((DIM,), jnp.float32)
        ln2_b = jnp.zeros((DIM,), jnp.float32)
        fc1_w = jax.random.normal(ks[5], (HID, DIM), jnp.float32) * 0.05
        fc1_b = jnp.zeros((HID,), jnp.float32)
        fc2_w = jax.random.normal(ks[6], (DIM, HID), jnp.float32) * 0.05
        fc2_b = jnp.zeros((DIM,), jnp.float32)
        return dict(x=x, adj=adj, W=W, a=a, fc_w=fc_w, fc_b=fc_b, ln1_g=ln1_g, ln1_b=ln1_b, ln2_g=ln2_g, ln2_b=ln2_b, fc1_w=fc1_w, fc1_b=fc1_b, fc2_w=fc2_w, fc2_b=fc2_b)
    _L0_gnn_all = _L0_gnn_setup()
    _L0_gnn_in = {k: v for k, v in _L0_gnn_all.items() if k in ('W', 'a', 'fc_w', 'fc_b', 'ln1_g', 'ln1_b', 'ln2_g', 'ln2_b', 'fc1_w', 'fc1_b', 'fc2_w', 'fc2_b', )}
    del _L0_gnn_all

    return {
        "x": x,
        "adj": adj,
        "L0_gnn_W": _L0_gnn_in["W"],
        "L0_gnn_a": _L0_gnn_in["a"],
        "L0_gnn_fc_w": _L0_gnn_in["fc_w"],
        "L0_gnn_fc_b": _L0_gnn_in["fc_b"],
        "L0_gnn_ln1_g": _L0_gnn_in["ln1_g"],
        "L0_gnn_ln1_b": _L0_gnn_in["ln1_b"],
        "L0_gnn_ln2_g": _L0_gnn_in["ln2_g"],
        "L0_gnn_ln2_b": _L0_gnn_in["ln2_b"],
        "L0_gnn_fc1_w": _L0_gnn_in["fc1_w"],
        "L0_gnn_fc1_b": _L0_gnn_in["fc1_b"],
        "L0_gnn_fc2_w": _L0_gnn_in["fc2_w"],
        "L0_gnn_fc2_b": _L0_gnn_in["fc2_b"],
    }

def reference(x, adj, L0_gnn_W, L0_gnn_a, L0_gnn_fc_w, L0_gnn_fc_b, L0_gnn_ln1_g, L0_gnn_ln1_b, L0_gnn_ln2_g, L0_gnn_ln2_b, L0_gnn_fc1_w, L0_gnn_fc1_b, L0_gnn_fc2_w, L0_gnn_fc2_b):
    import jax
    import jax.numpy as jnp
    def _L0_gnn_ref(x, adj, W, a, fc_w, fc_b, ln1_g, ln1_b, ln2_g, ln2_b, fc1_w, fc1_b, fc2_w, fc2_b):
        import jax, jax.numpy as jnp
        import numpy as np
        N, DIM = (4096, 512)
        F_OUT = DIM // 8
        HID = int(DIM * 2.0)
        ALPHA = 0.2
        MASK_VAL = -9000000000000000.0

        def _layernorm(x, g, b, eps=1e-05):
            mu = x.mean(-1, keepdims=True)
            var = ((x - mu) ** 2).mean(-1, keepdims=True)
            return (x - mu) * jax.lax.rsqrt(var + eps) * g + b
        h = _layernorm(x, ln1_g, ln1_b)
        Wh = h @ W
        f_src = Wh @ a[:F_OUT, 0]
        f_dst = Wh @ a[F_OUT:, 0]
        e = f_src[:, None] + f_dst[None, :]
        e = jnp.where(e >= 0, e, ALPHA * e)
        att = jax.nn.softmax(jnp.where(adj > 0, e, MASK_VAL), axis=1)
        h_prime = att @ Wh
        attn_out = h_prime @ fc_w.T + fc_b
        x = x + attn_out
        h2 = _layernorm(x, ln2_g, ln2_b)
        m = jax.nn.gelu(h2 @ fc1_w.T + fc1_b, approximate=False)
        m = m @ fc2_w.T + fc2_b
        return x + m

    x = _L0_gnn_ref(x, adj, L0_gnn_W, L0_gnn_a, L0_gnn_fc_w, L0_gnn_fc_b, L0_gnn_ln1_g, L0_gnn_ln1_b, L0_gnn_ln2_g, L0_gnn_ln2_b, L0_gnn_fc1_w, L0_gnn_fc1_b, L0_gnn_fc2_w, L0_gnn_fc2_b)
    return x


_drawn_inputs = setup_inputs


def setup_inputs(seed=0):
    import zlib

    import numpy as np

    out = dict(_drawn_inputs(seed))
    spreads = {'L0_gnn_fc_b': (0.0, 0.1),
     'L0_gnn_ln1_g': (1.0, 0.2),
     'L0_gnn_ln1_b': (0.0, 0.1),
     'L0_gnn_ln2_g': (1.0, 0.2),
     'L0_gnn_ln2_b': (0.0, 0.1),
     'L0_gnn_fc1_b': (0.0, 0.1),
     'L0_gnn_fc2_b': (0.0, 0.1)}
    factors = {}
    for name, (base, spread) in spreads.items():
        noise = np.random.default_rng([zlib.crc32(name.encode()), seed]).standard_normal(out[name].shape)
        drawn = base * np.exp(spread * noise) if base else spread * noise
        out[name] = jnp.asarray(drawn.astype(out[name].dtype))
    for name, factor in factors.items():
        out[name] = (out[name] * factor).astype(out[name].dtype)
    return out
```

```python
from contextlib import ExitStack

import numpy as np

import concourse.bass as bass
from concourse import mybir

ALU = mybir.AluOpType
ACT = mybir.ActivationFunctionType
AX_X = mybir.AxisListType.X
RMAX = bass.bass_isa.ReduceOp.max
F32 = mybir.dt.float32
F32R = mybir.dt.float32r
BF16 = mybir.dt.bfloat16
I32 = mybir.dt.int32

P = 128
N = 8192
D = 512
F = D // 8
HID = 2 * D
SLOPE = 0.2
EPS = 1e-5
KT = D // P
HT = HID // P
NT = N // P
BLK = 512
NB = N // BLK
TB = BLK // P
PAIR = 2
NQ = NT // PAIR
RA = 4
RM = 2
SUB = 256
NS = BLK // SUB
TS = SUB // P

GROUP_CHAIN = 2
EPI_CHAIN = 7
MLP_CHAIN = 2


def gat_layer(nc, x, adj_tiles, w, a, fc_wt, fc_b, ln1_g, ln1_b, ln2_g, ln2_b,
              fc1_wt, fc1_b, fc2_wt, fc2_b, ident_in, out):
    ctx = ExitStack()
    with ctx:
        def sb(name, shape, dt):
            return ctx.enter_context(nc.sbuf_tensor(name, shape, dt))

        def bank(name):
            return ctx.enter_context(nc.psum_tensor(name, [P, 512], F32))

        def sem(name):
            return ctx.enter_context(nc.semaphore(name))

        wpos = sb("wpos", [P, NT, 2 * F], F32R)
        wneg = sb("wneg", [P, NT, 2 * F], F32R)
        fc1_hi = sb("fc1_hi", [P, KT, HID], F32R)
        fc1_lo = sb("fc1_lo", [P, KT, HID], F32R)
        fc2_hi = sb("fc2_hi", [P, HT, D], F32R)
        fc2_lo = sb("fc2_lo", [P, HT, D], F32R)
        mpos = sb("mpos", [P, RM, PAIR * BLK], F32R)
        mneg = sb("mneg", [P, RM, PAIR * BLK], F32R)
        h2_hi = sb("h2_hi", [P, KT, SUB], F32R)
        h2_lo = sb("h2_lo", [P, KT, SUB], F32R)
        m_hi = sb("m_hi", [P, 2, SUB], F32R)
        m_lo = sb("m_lo", [P, 2, SUB], F32R)
        fcw2 = sb("fcw2", [P, D], F32)
        bias_rows = sb("bias_rows", [P, 2, D], F32)
        fcb_bc = bias_rows[:, 0, :]
        fc2b_bc = bias_rows[:, 1, :]
        ident = sb("ident", [P, P], F32)
        ones = sb("ones", [P, P], F32)
        negd = sb("negd", [P, NT], F32)
        den_pos = sb("den_pos", [P, NT, 3], BF16)
        den_neg = sb("den_neg", [P, NT, 3], BF16)
        mean_wh = sb("mean_wh", [P, 1], F32)
        fc1_bias = sb("fc1_bias", [P, HT], F32)
        stats = sb("stats", [P, TB, 6], F32)
        mv = sb("mv", [P, TB, 2], F32)
        var_eps = sb("var_eps", [P, TB], F32)
        minus_half = sb("minus_half", [P, TB], F32)
        rstd = sb("rstd", [P, TB], F32)

        KIB = 256
        arena = sb("arena", [P, 42 * KIB], F32)

        def part(start, kib):
            return arena[:, start * KIB:(start + kib) * KIB]

        stage1 = part(0, 16).rearrange("p (k n) -> p k n", k=KT)
        stage2 = part(16, 16).rearrange("p (k n) -> p k n", k=HT)
        xin = [part(8 * i, 8).rearrange("p (t n) -> p t n", t=TB) for i in range(2)]
        ht = part(16, 8).rearrange("p (k n) -> p k n", k=KT)
        wht = part(24, 2)
        wh_all = part(26, 16).rearrange("p (t f) -> p t f", t=NT)
        full = part(0, 16).rearrange("p (t f) -> p t f", t=NT)
        sact = part(16, 2)[0:NT, 0:3 * P].rearrange("p (c n) -> p c n", c=3)
        adj_ring = part(0, 16).bitcast(I32).rearrange("p (r n) -> p r n", r=RA)
        sign_ring = part(16, 4).bitcast(BF16).rearrange("p (r n) -> p r n", r=RM)
        s_bc = part(20, 4).rearrange("p (r n) -> p r n", r=2)
        a_bc = part(24, 2)
        c_bc = part(26, 2)
        tmp = part(28, 2)
        comb = part(30, 2)
        x2 = part(32, 4).rearrange("p (t n) -> p t n", t=TS)
        xn = part(36, 2)
        gl = part(38, 2).rearrange("p (r n) -> p r n", r=2)

        small = bias_rows[:, :, :].rearrange("p a n -> p (a n)")
        wsb = small[:, 0:KT * F].rearrange("p (k f) -> p k f", k=KT)
        a2 = sb("a2", [F, 2], F32)
        g1 = sb("g1", [P, KT], F32)
        b1 = sb("b1", [P, KT], F32)
        g2 = sb("g2", [P, KT], F32)
        b2 = sb("b2", [P, KT], F32)
        fc1b = sb("fc1b", [P, HT], F32)
        small = small[:, KT * F:].rearrange("p (a n) -> p a n", n=NT)
        sd = small[:, 0:2, :]
        sac = small[:, 2:5, :]
        cols = small[:, 5:9, :]
        bd = small[:, 9:11, :]
        dmax = sb("dmax", [P, 2], F32)

        sac_dram = nc.dram_tensor("sac_dram", (3, N), F32, kind="Internal").ap()

        banks = [bank(f"bank{i}") for i in range(8)]
        ps_t = banks[0:4]
        ps_wht, ps_whj, ps_sd, ps_misc = banks[4:8]
        ps_pos, ps_neg, ps_den, ps_x = banks[0:4]
        ps_f = banks[4:6]
        ps_y = banks[6:8]

        consts_in = sem("consts_in")
        stage_in = [sem("stage1_in"), sem("stage2_in")]
        rows_in = sem("rows_in")
        carrier = sem("carrier")
        pool_carrier = sem("pool_carrier")
        consts_set = sem("consts_set")
        prep_chain = sem("prep_chain")
        bias_mm = sem("bias_mm")
        prep_done = sem("prep_done")
        xin_in = [sem("xin_in0"), sem("xin_in1")]
        xin_free = sem("xin_free")
        group_chain = sem("group_chain")
        var1 = sem("var1")
        rstd1 = sem("rstd1")
        xn1 = sem("xn1")
        xt1 = sem("xt1")
        h1 = sem("h1")
        wht_ps = sem("wht_ps")
        wht_sb = sem("wht_sb")
        whj_ps = sem("whj_ps")
        whj_sb = sem("whj_sb")
        dmax_part = sem("dmax_part")
        dmax_all = sem("dmax_all")
        cols_set = sem("cols_set")
        exps_set = sem("exps_set")
        sact_ps = sem("sact_ps")
        sact_sb = sem("sact_sb")
        sac_out = sem("sac_out")
        mean_ps = sem("mean_ps")
        split_chain = sem("split_chain")
        phase1_done = sem("phase1_done")

        adj_in = [sem(f"adj_in{i}") for i in range(RA)]
        adj_free = sem("adj_free")
        s_in = [sem("s_in0"), sem("s_in1")]
        s_free = sem("s_free")
        ac_in = sem("ac_in")
        ac_free = sem("ac_free")
        sign_made = sem("sign_made")
        signed = sem("signed")
        masks = sem("masks")
        masks_free = sem("masks_free")
        attn_ps = sem("attn_ps")
        attn_ps_free = sem("attn_ps_free")
        epi_chain = sem("epi_chain")
        den_parts = sem("den_parts")
        den_sum = sem("den_sum")
        den_read = sem("den_read")
        comb_made = sem("comb_made")
        comb_free = sem("comb_free")
        x_in = sem("x_in")
        fc_ps = sem("fc_ps")
        x2_part = sem("x2_part")
        x2_made = sem("x2_made")
        mlp_chain = sem("mlp_chain")
        var2 = sem("var2")
        rstd2 = sem("rstd2")
        xn2 = sem("xn2")
        xt2 = sem("xt2")
        h2hi_made = sem("h2hi_made")
        h2_made = sem("h2_made")
        f_ps = sem("f_ps")
        gelu_made = sem("gelu_made")
        mhi_made = sem("mhi_made")
        m_made = sem("m_made")
        m_free = sem("m_free")
        y_ps = sem("y_ps")
        y_part = sem("y_part")
        y_made = sem("y_made")
        out_done = sem("out_done")

        block = ctx.enter_context(nc.Block())

        CONSTS = 10

        @block.sync
        def _(sp):
            sp.dma_start(stage1, fc1_wt.rearrange("(k p) n -> p k n", p=P)).then_inc(stage_in[0], 16)
            sp.dma_start(stage2, fc2_wt.rearrange("(k p) n -> p k n", p=P)).then_inc(stage_in[1], 16)
            for dst, src in ((ident[:, :], ident_in),
                             (wsb, w.rearrange("(k p) n -> p k n", p=P)),
                             (a2[:, :], a),
                             (g1[:, :], ln1_g), (b1[:, :], ln1_b), (g2[:, :], ln2_g), (b2[:, :], ln2_b),
                             (fc1b[:, :], fc1_b),
                             (fcw2[0:F, :], fc_wt), (fcw2[F:P, :], fc_wt)):
                sp.dma_start(dst, src).then_inc(consts_in, 16)

            xg = x.rearrange("(g t p) n -> g p t n", t=TB, p=P)
            sp.wait_ge(prep_done, 1)
            with sp.Fori(0, NB // 2) as gi:
                for par in range(2):
                    g = gi * 2 + par
                    sp.wait_ge(xin_free, g + 1)
                    sp.dma_start(xin[par], xg[bass.ds(g, 1)].rearrange("g p t n -> (g p) t n")
                                 ).then_inc(xin_in[par], 16)

            sp.wait_ge(sact_sb, 3)
            for c in range(3):
                sp.dma_start(sac_dram[c].rearrange("(t p) -> t p", p=P), sact[:, c, :]).then_inc(sac_out, 16)
            sp.wait_ge(sac_out, 48)
            sp.wait_ge(phase1_done, 1)
            sp.dma_start(fcb_bc, fc_b.broadcast_to([P, D])).then_inc(rows_in, 16)
            sp.dma_start(fc2b_bc, fc2_b.broadcast_to([P, D])).then_inc(rows_in, 16)
            sp.dma_start(s_bc[:, 0, :], sac_dram[0:1, 0:BLK].broadcast_to([P, BLK])).then_inc(s_in[0], 16)
            with sp.Fori(0, NB // 2) as bi:
                for par in range(2):
                    ib = bi * 2 + par
                    for q in range(NQ):
                        sp.wait_ge(adj_free, ib * NQ + (q + 1))
                        sp.dma_start(adj_ring[:, q % RA, :],
                                     adj_tiles[bass.ds(ib, 1), q].rearrange("b p n -> (b p) n")
                                     ).then_inc(adj_in[q % RA], 16)
                        if q == RA:
                            sp.wait_ge(ac_free, ib + 1)
                            for c, dst in ((1, a_bc), (2, c_bc)):
                                sp.dma_start(dst, sac_dram[c:c + 1, bass.ds(ib * BLK, BLK)]
                                             .broadcast_to([P, BLK])).then_inc(ac_in, 16)
                            sp.wait_ge(s_free, ib + 1)
                            nxt = (bi * 2 + 1) if par == 0 else (bi * 2 + 2) % NB
                            sp.dma_start(s_bc[:, 1 - par, :], sac_dram[0:1, bass.ds(nxt * BLK, BLK)]
                                         .broadcast_to([P, BLK])).then_inc(s_in[1 - par], 16)
            sp.wait_ge(s_in[0], (NB // 2 + 1) * 16)

        @block.gpsimd
        def _(pool):
            pool.memset(ones[:, :], 1.0).then_inc(consts_set, 1)
            pool.memset(minus_half[:, :], -0.5).then_inc(consts_set, 1)
            pool.wait_ge(consts_set, 3)
            with pool.Fori(0, NB) as g:
                pool.wait_ge(var1, g + 1)
                pool.tensor_tensor(rstd[:, :], var_eps[:, :], minus_half[:, :], ALU.pow).then_inc(rstd1, 1)
            pool.wait_ge(dmax_part, 1)
            pool.partition_all_reduce(dmax[:, 1:2], dmax[:, 0:1], P, RMAX).then_inc(dmax_all, 1)

            pool.wait_ge(phase1_done, 1)
            pool.wait_ge(rows_in, 32)
            xs = x.rearrange("(n t p) d -> n p t d", t=TS, p=P)
            os_ = out.rearrange("(n t p) d -> n p t d", t=TS, p=P)
            with pool.Fori(0, NB) as ib:
                for sbk in range(NS):
                    n = ib * NS + sbk
                    pool.dma_start(x2, xs[bass.ds(n, 1)].rearrange("n p t d -> (n p) t d")).then_inc(x_in, 16)
                    for t in range(TS):
                        pool.wait_ge(x2_part, n * TS + (t + 1))
                        pool.tensor_tensor(x2[:, t, :], x2[:, t, :], fcb_bc, ALU.add).then_inc(x2_made, 1)
                        pool.wait_ge(var2, n * TS + (t + 1))
                        pool.tensor_tensor(rstd[:, t:t + 1], var_eps[:, t:t + 1], minus_half[:, t:t + 1],
                                           ALU.pow).then_inc(rstd2, 1)
                    for t in range(TS):
                        pool.wait_ge(y_part, n * TS + (t + 1 + TS))
                        pool.tensor_tensor(x2[:, t, :], x2[:, t, :], fc2b_bc, ALU.add).then_inc(y_made, 1)
                    pool.wait_ge(y_made, n * TS + TS)
                    pool.sem_inc(pool_carrier, 1)
                    pool.dma_start(os_[bass.ds(n, 1)].rearrange("n p t d -> (n p) t d"), x2).then_inc(out_done, 16)
                    pool.wait_ge(out_done, n * 16 + 16)

        @block.scalar
        def _(act):
            act.sem_inc(masks, 2 * RM)
            act.sem_inc(whj_sb, 2)
            act.sem_inc(gelu_made, 2)
            act.wait_ge(consts_in, 16 * CONSTS)
            with act.Fori(0, NB) as g:
                for k in range(KT):
                    act.wait_ge(xt1, g * KT + (k + 1))
                    if k == 0:
                        act.wait_ge(wht_ps, g + 1)
                    act.activation(ht[:, k, :], ps_t[k][:, :], ACT.Identity, bias=b1[:, k:k + 1],
                                   scale=g1[:, k:k + 1]).then_inc(h1, 1)
                act.wait_ge(wht_ps, g + 2)
                act.copy(wht[0:F, :], ps_wht[0:F, :]).then_inc(wht_sb, 1)
                act.wait_ge(whj_ps, g + 1)
                act.copy(wh_all[:, bass.ds(g * TB, TB), :],
                         ps_whj[:, 0:TB * F].rearrange("p (t f) -> p t f", t=TB)).then_inc(whj_sb, 1)
                act.copy(sd[:, :, bass.ds(g * TB, TB)],
                         ps_sd[:, 0:2 * TB].rearrange("p (t c) -> p c t", c=2)).then_inc(whj_sb, 1)
            act.wait_ge(cols_set, 4)
            act.activation(bd[:, 0, :], cols[:, 0, :], ACT.Exp).then_inc(exps_set, 1)
            act.activation(bd[:, 1, :], cols[:, 0, :], ACT.Exp, scale=SLOPE).then_inc(exps_set, 1)
            act.activation(sac[:, 1, :], cols[:, 2, :], ACT.Exp, scale=1 - SLOPE).then_inc(exps_set, 1)
            act.activation(sac[:, 2, :], cols[:, 3, :], ACT.Exp, scale=SLOPE - 1).then_inc(exps_set, 1)
            act.copy(sac[:, 0, :], sd[:, 0, :]).then_inc(exps_set, 1)
            act.wait_ge(sact_ps, 1)
            for c in range(3):
                act.copy(sact[:, c, :], ps_misc[0:NT, c * P:(c + 1) * P]).then_inc(sact_sb, 1)

            act.wait_ge(phase1_done, 1)
            with act.Fori(0, NB) as ib:
                for q in range(NQ):
                    act.wait_ge(signed, ib * NQ + (q + 1))
                    act.wait_ge(masks_free, ib * NQ + (q + 1))
                    src = sign_ring[:, q % RM, :]
                    act.activation(mpos[:, q % RM, :], src, ACT.Relu, scale=2.0).then_inc(masks, 1)
                    act.activation(mneg[:, q % RM, :], src, ACT.Relu, scale=-2.0).then_inc(masks, 1)
                for sbk in range(NS):
                    n = ib * NS + sbk
                    for t in range(TS):
                        act.wait_ge(xt2, n * TS + (t + 2))
                        if t == 0:
                            act.wait_ge(f_ps, n * HT + 1)
                        act.copy(h2_hi[:, :, t * P:(t + 1) * P],
                                 ps_x[:, :].rearrange("p (k n) -> p k n", k=KT)).then_inc(h2hi_made, 1)
                    for h in range(HT):
                        act.wait_ge(f_ps, n * HT + (h + 2))
                        act.wait_ge(m_made, n * HT + (h + 1))
                        act.activation(gl[:, h % 2, :], ps_f[h % 2][:, 0:SUB], ACT.Gelu,
                                       bias=fc1_bias[:, h:h + 1]).then_inc(gelu_made, 1)

        @block.vector
        def _(dve):
            dve.memset(mean_wh[:, :], 0.0).then_inc(consts_set, 1)
            dve.sem_inc(xin_free, 2)
            dve.sem_inc(adj_free, RA)
            dve.sem_inc(ac_free, 1)
            dve.sem_inc(s_free, 1)
            dve.sem_inc(m_made, 2)
            dve.sem_inc(attn_ps_free, 1)
            dve.sem_inc(y_part, TS)
            dve.sem_inc(h2_made, 1)

            dve.wait_ge(consts_in, 16 * CONSTS)
            dve.wait_ge(stage_in[0], 16)
            dve.wait_ge(bias_mm, 1)
            dve.tensor_tensor(fc1_bias[:, :], ps_misc[:, 0:HT], fc1b[:, :], ALU.add).then_inc(prep_chain, 1)
            for k in range(KT):
                dve.tensor_scalar(stage1[:, k, :], stage1[:, k, :], g2[:, k:k + 1], None, ALU.mult
                                  ).then_inc(prep_chain, 1)
            dve.wait_ge(prep_chain, 5)
            dve.tensor_copy(fc1_hi[:, :, :], stage1).then_inc(prep_chain, 1)
            dve.wait_ge(stage_in[1], 16)
            dve.tensor_copy(fc2_hi[:, :, :], stage2).then_inc(prep_chain, 1)
            dve.wait_ge(prep_chain, 7)
            dve.tensor_tensor(fc1_lo[:, :, :], stage1, fc1_hi[:, :, :].bitcast(F32), ALU.subtract
                              ).then_inc(prep_chain, 1)
            dve.tensor_tensor(fc2_lo[:, :, :], stage2, fc2_hi[:, :, :].bitcast(F32), ALU.subtract
                              ).then_inc(prep_chain, 1)
            dve.wait_ge(prep_chain, 9)
            dve.sem_inc(prep_done, 1)

            with dve.Fori(0, NB // 2) as gi:
                for par in range(2):
                    g = gi * 2 + par
                    base = g * GROUP_CHAIN
                    dve.wait_ge(xin_in[par], gi * 16 + 16)
                    for t in range(TB):
                        ins = dve.bn_stats(stats[:, t, :], xin[par][:, t, :])
                    ins.then_inc(group_chain, 1)
                    dve.wait_ge(group_chain, base + 1)
                    dve.sem_inc(carrier, 1)
                    for t in range(TB):
                        ins = dve.bn_aggr(mv[:, t, :], stats[:, t, :])
                    ins.then_inc(group_chain, 1)
                    dve.wait_ge(group_chain, base + 2)
                    dve.tensor_scalar(var_eps[:, :], mv[:, :, 1], EPS, None, ALU.add).then_inc(var1, 1)
                    dve.wait_ge(rstd1, g + 1)
                    for t in range(TB):
                        ins = dve.tensor_scalar(xin[par][:, t, :], xin[par][:, t, :], mv[:, t, 0:1],
                                                rstd[:, t:t + 1], ALU.subtract, ALU.mult)
                    ins.then_inc(xn1, 1)

            dve.wait_ge(whj_sb, 2 * NB + 2)
            dve.tensor_reduce(dmax[:, 0:1], sd[:, 1, :], AX_X, ALU.max).then_inc(dmax_part, 1)
            dve.tensor_scalar(negd[:, :], sd[:, 1, :], -1.0, None, ALU.mult).then_inc(split_chain, 1)
            dve.wait_ge(dmax_all, 1)
            dve.tensor_scalar(cols[:, 0, :], sd[:, 1, :], dmax[:, 1:2], None, ALU.subtract).then_inc(cols_set, 1)
            dve.tensor_scalar(cols[:, 1, :], sd[:, 0, :], dmax[:, 1:2], None, ALU.add).then_inc(cols_set, 1)
            dve.tensor_scalar(cols[:, 2, :], sd[:, 0, :], dmax[:, 1:2], 0.0, ALU.add, ALU.min).then_inc(cols_set, 1)
            dve.tensor_scalar(cols[:, 3, :], sd[:, 0, :], dmax[:, 1:2], 0.0, ALU.add, ALU.max).then_inc(cols_set, 1)
            dve.wait_ge(exps_set, 2)
            step = 1
            for c, wdst, ddst in ((0, wpos, den_pos), (1, wneg, den_neg)):
                fac = bd[:, c, :]
                dve.tensor_tensor(full, wh_all, fac.unsqueeze(2).broadcast_to([P, NT, F]), ALU.mult
                                  ).then_inc(split_chain, 1)
                dve.tensor_copy(ddst[:, :, 0], fac).then_inc(split_chain, 1)
                step += 2
                dve.wait_ge(split_chain, step)
                dve.tensor_copy(wdst[:, :, 0:F], full).then_inc(split_chain, 1)
                dve.wait_ge(exps_set, 5)
                dve.tensor_tensor(cols[:, 0, :], fac, ddst[:, :, 0], ALU.subtract).then_inc(split_chain, 1)
                step += 2
                dve.wait_ge(split_chain, step)
                dve.tensor_tensor(wdst[:, :, F:2 * F], full, wdst[:, :, 0:F].bitcast(F32), ALU.subtract
                                  ).then_inc(split_chain, 1)
                dve.tensor_copy(ddst[:, :, 1], cols[:, 0, :]).then_inc(split_chain, 1)
                step += 2
                dve.wait_ge(split_chain, step)
                dve.tensor_tensor(ddst[:, :, 2], cols[:, 0, :], ddst[:, :, 1], ALU.subtract).then_inc(split_chain, 1)
                step += 1
            dve.wait_ge(mean_ps, 1)
            dve.tensor_scalar(mean_wh[0:F, :], ps_wht[0:F, 0:1], 1.0 / N, None, ALU.mult).then_inc(split_chain, 1)
            dve.memset(ps_den[:, :], 0.0).then_inc(split_chain, 1)
            dve.wait_ge(split_chain, step + 2)
            dve.wait_ge(sac_out, 48)
            dve.sem_inc(phase1_done, 1)

            def sign(ib, par, q):
                dve.wait_ge(masks, ib * (2 * NQ) + (2 * q + 2))
                for u in range(PAIR):
                    j = PAIR * q + u
                    ins = dve.tensor_scalar(sign_ring[:, q % RM, u * BLK:(u + 1) * BLK], s_bc[:, par, :],
                                            negd[:, j:j + 1], 0.5, ALU.is_ge, ALU.subtract)
                ins.then_inc(sign_made, 1)
                if q == NQ - 1:
                    dve.wait_ge(sign_made, ib * NQ + NQ)
                    dve.sem_inc(s_free, 1)

            def mask_sign(ib, par, bi, q):
                k = ib * NQ + q
                dve.wait_ge(sign_made, k + 1)
                dve.wait_ge(adj_in[q % RA], ib * (16 * NQ // RA) + 16 * (q // RA + 1))
                dve.scalar_tensor_tensor(out=sign_ring[:, q % RM, :], in0=adj_ring[:, q % RA, :], scalar=0.0,
                                         in1=sign_ring[:, q % RM, :], op0=ALU.is_gt, op1=ALU.mult
                                         ).then_inc(signed, 1)
                dve.wait_ge(signed, k + 1)
                dve.sem_inc(adj_free, 1)

            def epilogue(ib):
                e = ib * EPI_CHAIN
                dve.wait_ge(attn_ps, ib + 1)
                dve.wait_ge(ac_in, ib * 32 + 32)
                dve.wait_ge(comb_free, ib + 1)
                dve.tensor_tensor(comb, a_bc, ps_pos[:, :], ALU.mult).then_inc(epi_chain, 1)
                dve.tensor_tensor(tmp, c_bc, ps_neg[:, :], ALU.mult).then_inc(epi_chain, 1)
                dve.wait_ge(epi_chain, e + 1)
                h = P // 2
                dve.tensor_tensor(a_bc[0:h, :], a_bc[0:h, :], ps_den[0:h, :], ALU.mult).then_inc(den_parts, 1)
                dve.tensor_tensor(a_bc[h:P, :], c_bc[h:P, :], ps_den[h:P, :], ALU.mult).then_inc(den_parts, 1)
                dve.wait_ge(epi_chain, e + 2)
                dve.tensor_tensor(comb, comb, tmp, ALU.add).then_inc(epi_chain, 1)
                dve.wait_ge(den_parts, ib * 2 + 2)
                dve.sem_inc(attn_ps_free, 1)
                dve.wait_ge(den_sum, ib + 1)
                dve.tensor_scalar(c_bc, ps_x[:, :], 0.0, None, ALU.is_equal).then_inc(epi_chain, 1)
                dve.wait_ge(epi_chain, e + 4)
                dve.tensor_tensor(tmp, c_bc, ps_x[:, :], ALU.add).then_inc(epi_chain, 1)
                dve.wait_ge(epi_chain, e + 5)
                dve.reciprocal(tmp, tmp).then_inc(epi_chain, 1)
                dve.wait_ge(epi_chain, e + 6)
                dve.tensor_tensor(comb, comb, tmp, ALU.mult).then_inc(epi_chain, 1)
                dve.wait_ge(epi_chain, e + 7)
                dve.scalar_tensor_tensor(out=comb, in0=c_bc, scalar=mean_wh[:, 0:1], in1=comb,
                                         op0=ALU.mult, op1=ALU.add).then_inc(comb_made, 1)
                dve.wait_ge(comb_made, ib + 1)
                dve.sem_inc(ac_free, 1)

            def mlp(n):
                for t in range(TS):
                    dve.wait_ge(x_in, n * 16 + 16)
                    dve.wait_ge(fc_ps, n * TS + (t + 1))
                    dve.tensor_tensor(x2[:, t, :], ps_y[t][:, :], x2[:, t, :], ALU.add).then_inc(x2_part, 1)
                for t in range(TS):
                    c = n * (TS * MLP_CHAIN) + t * MLP_CHAIN
                    dve.wait_ge(x2_made, n * TS + (t + 1))
                    dve.bn_stats(stats[:, t, :], x2[:, t, :]).then_inc(mlp_chain, 1)
                    dve.wait_ge(mlp_chain, c + 1)
                    dve.sem_inc(carrier, 1)
                    dve.bn_aggr(mv[:, t, :], stats[:, t, :]).then_inc(mlp_chain, 1)
                    dve.wait_ge(mlp_chain, c + 2)
                    dve.tensor_scalar(var_eps[:, t:t + 1], mv[:, t, 1:2], EPS, None, ALU.add).then_inc(var2, 1)
                for t in range(TS):
                    dve.wait_ge(rstd2, n * TS + (t + 1))
                    dve.wait_ge(xt2, n * TS + (t + 1))
                    dve.tensor_scalar(xn, x2[:, t, :], mv[:, t, 0:1], rstd[:, t:t + 1], ALU.subtract, ALU.mult
                                      ).then_inc(xn2, 1)
                for t in range(TS):
                    dve.wait_ge(h2hi_made, n * TS + (t + 1))
                    dve.tensor_tensor(h2_lo[:, :, t * P:(t + 1) * P],
                                      ps_x[:, :].rearrange("p (k n) -> p k n", k=KT),
                                      h2_hi[:, :, t * P:(t + 1) * P].bitcast(F32), ALU.subtract
                                      ).then_inc(h2_made, 1)
                for h in range(HT):
                    dve.wait_ge(gelu_made, n * HT + (h + 3))
                    dve.wait_ge(m_free, n * HT + (h + 1))
                    dve.tensor_copy(m_hi[:, h % 2, :], gl[:, h % 2, :]).then_inc(mhi_made, 1)
                    dve.wait_ge(mhi_made, n * HT + (h + 1))
                    dve.tensor_tensor(m_lo[:, h % 2, :], gl[:, h % 2, :], m_hi[:, h % 2, :].bitcast(F32),
                                      ALU.subtract).then_inc(m_made, 1)
                dve.wait_ge(y_ps, n + 1)
                for t in range(TS):
                    dve.tensor_tensor(x2[:, t, :], ps_y[t][:, :], x2[:, t, :], ALU.add).then_inc(y_part, 1)

            with dve.Fori(0, NB // 2) as bi:
                for par in range(2):
                    ib = bi * 2 + par
                    dve.wait_ge(s_in[par], bi * 16 + 16)
                    sign(ib, par, 0)
                    for q in range(NQ):
                        if q + 1 < NQ:
                            sign(ib, par, q + 1)
                        mask_sign(ib, par, bi, q)
                    epilogue(ib)
                    for sbk in range(NS):
                        mlp(ib * NS + sbk)

        @block.tensor
        def _(pe):
            pe.sem_inc(wht_ps, 1)
            pe.sem_inc(masks_free, RM)
            pe.sem_inc(f_ps, 1)
            pe.sem_inc(m_free, 2)
            pe.sem_inc(comb_free, 1)
            pe.sem_inc(xt2, 1)
            pe.wait_ge(consts_in, 16 * CONSTS)
            pe.wait_ge(stage_in[0], 16)
            for h in range(HT):
                for k in range(KT):
                    ins = pe.matmul(ps_misc[:, h:h + 1], stage1[:, k, h * P:(h + 1) * P], b2[:, k:k + 1],
                                    start=(k == 0), stop=(k == KT - 1))
            ins.then_inc(bias_mm, 1)

            with pe.Fori(0, NB // 2) as gi:
                for par in range(2):
                    g = gi * 2 + par
                    pe.wait_ge(xn1, g + 1)
                    for k in range(KT):
                        for t in range(TB):
                            ins = pe.transpose(ps_t[k][:, t * P:(t + 1) * P], xin[par][:, t, k * P:(k + 1) * P],
                                               ident[:, :])
                        ins.then_inc(xt1, 1)
                    pe.wait_ge(xt1, g * KT + KT)
                    pe.sem_inc(xin_free, 1)
                    for k in range(KT):
                        pe.wait_ge(h1, g * KT + (k + 1))
                        ins = pe.matmul(ps_wht[0:F, :], wsb[:, k, :], ht[:, k, :], start=(k == 0), stop=(k == KT - 1))
                    ins.then_inc(wht_ps, 1)
                    pe.wait_ge(wht_sb, g + 1)
                    pe.wait_ge(whj_sb, g * 2 + 2)
                    for t in range(TB):
                        pe.matmul(ps_sd[:, 2 * t:2 * t + 2], wht[0:F, t * P:(t + 1) * P], a2[:, :],
                                  start=True, stop=True)
                        ins = pe.transpose(ps_whj[:, t * F:(t + 1) * F], wht[0:F, t * P:(t + 1) * P],
                                           ident[0:F, 0:F])
                    ins.then_inc(whj_ps, 1)

            pe.wait_ge(exps_set, 5)
            for c in range(3):
                ins = pe.transpose(ps_misc[0:NT, c * P:(c + 1) * P], sac[:, c, :], ident[:, :])
            ins.then_inc(sact_ps, 1)
            pe.wait_ge(consts_set, 3)
            for t in range(NT):
                ins = pe.matmul(ps_wht[0:F, 0:1], wh_all[:, t, :], ones[:, 0:1], start=(t == 0), stop=(t == NT - 1))
            ins.then_inc(mean_ps, 1)

            def attention(ib, q):
                pe.wait_ge(masks, ib * (2 * NQ) + (2 * q + 6))
                if q == 0:
                    pe.wait_ge(attn_ps_free, ib + 1)
                r = q % RM
                for u in range(PAIR):
                    j = PAIR * q + u
                    cut = slice(u * BLK, (u + 1) * BLK)
                    pe.matmul(ps_pos[:, :], wpos[:, j, :], mpos[:, r, cut], start=(j == 0), stop=(j == NT - 1))
                    pe.matmul(ps_neg[:, :], wneg[:, j, :], mneg[:, r, cut], start=(j == 0), stop=(j == NT - 1))
                for c, (m, dw) in enumerate(((mpos, den_pos), (mneg, den_neg))):
                    for u in range(PAIR):
                        j = PAIR * q + u
                        o = 32 * (2 * c + u)
                        half = m[:, r, u * BLK:(u + 1) * BLK].bitcast(BF16)[:, 1::2]
                        ins = pe.matmul(ps_den[o:o + 3, :], dw[:, j, :], half, start=(q == 0), stop=(q == NQ - 1),
                                        tile_position=(0, o))
                ins.then_inc(masks_free, 1)
                if q == NQ - 1:
                    ins = pe.wait_ge(masks_free, ib * NQ + (NQ + RM))
                    pe.sem_inc(attn_ps, 1)

            def denominator(ib):
                pe.wait_ge(den_parts, ib * 2 + 2)
                pe.matmul(ps_x[:, :], ones[:, :], a_bc, start=True, stop=True).then_inc(den_sum, 1)

            def mlp(ib, sbk):
                n = ib * NS + sbk
                pe.wait_ge(comb_made, ib + 1)
                pe.wait_ge(y_part, n * TS + TS)
                for t in range(TS):
                    c = (sbk * TS + t) * P
                    pe.matmul(ps_y[t][:, :], comb[:, c:c + P], fcw2[:, :], start=True, stop=True).then_inc(fc_ps, 1)
                if sbk == NS - 1:
                    pe.wait_ge(fc_ps, n * TS + TS)
                    pe.sem_inc(comb_free, 1)
                for t in range(TS):
                    pe.wait_ge(xn2, n * TS + (t + 1))
                    pe.wait_ge(h2_made, n * TS + (t + 1))
                    for k in range(KT):
                        ins = pe.transpose(ps_x[:, k * P:(k + 1) * P], xn[:, k * P:(k + 1) * P], ident[:, :])
                    ins.then_inc(xt2, 1)
                pe.wait_ge(h2_made, n * TS + (TS + 1))

                def fc1(h):
                    pe.wait_ge(gelu_made, n * HT + (h + 1))
                    cut = slice(h * P, (h + 1) * P)
                    i = 0
                    for wt, v in ((fc1_hi, h2_hi), (fc1_lo, h2_hi), (fc1_hi, h2_lo)):
                        for k in range(KT):
                            ins = pe.matmul(ps_f[h % 2][:, 0:SUB], wt[:, k, cut], v[:, k, :],
                                            start=(i == 0), stop=(i == 3 * KT - 1))
                            i += 1
                    ins.then_inc(f_ps, 1)

                def fc2(h):
                    pe.wait_ge(m_made, n * HT + (h + 3))
                    for t in range(TS):
                        cut = slice(t * P, (t + 1) * P)
                        for i, (m, wt) in enumerate(((m_hi, fc2_hi), (m_hi, fc2_lo), (m_lo, fc2_hi))):
                            ins = pe.matmul(ps_y[t][:, :], m[:, h % 2, cut], wt[:, h, :],
                                            start=(h == 0 and i == 0), stop=(h == HT - 1 and i == 2))
                    ins.then_inc(m_free, 1)

                fc1(0)
                for h in range(HT):
                    if h + 1 < HT:
                        fc1(h + 1)
                    if h == 0:
                        pe.wait_ge(x2_part, n * TS + TS)
                    fc2(h)
                pe.wait_ge(m_free, n * HT + (HT + 2))
                pe.sem_inc(y_ps, 1)

            pe.wait_ge(phase1_done, 1)
            with pe.Fori(0, NB) as ib:
                for q in range(NQ):
                    attention(ib, q)
                denominator(ib)
                for sbk in range(NS):
                    mlp(ib, sbk)


def kernel(**inputs):
    import concourse.bacc as bacc
    from concourse.bass_utils import run_bass_kernel_spmd

    nc = bacc.Bacc("TRN2", target_bir_lowering=False, num_devices=1)
    g = {k.replace("L0_gnn_", ""): np.asarray(v) for k, v in inputs.items()}
    adj = g["adj"].reshape(NB, BLK, NQ, PAIR, P).transpose(0, 2, 4, 3, 1).reshape(NB, NQ, P, PAIR * BLK)

    def columns(v):
        return v.reshape(-1, P).T

    arrays = {
        "x": g["x"], "adj_tiles": adj, "w": g["W"], "a": g["a"].reshape(2, F).T,
        "fc_wt": g["fc_w"].T, "fc_b": g["fc_b"].reshape(1, D),
        "ln1_g": columns(g["ln1_g"]), "ln1_b": columns(g["ln1_b"]),
        "ln2_g": columns(g["ln2_g"]), "ln2_b": columns(g["ln2_b"]),
        "fc1_wt": g["fc1_w"].T, "fc1_b": columns(g["fc1_b"]),
        "fc2_wt": g["fc2_w"].T, "fc2_b": g["fc2_b"].reshape(1, D),
        "ident_in": np.eye(P, dtype=np.float32),
    }
    arrays = {k: np.ascontiguousarray(v) for k, v in arrays.items()}
    aps = {k: nc.dram_tensor("in_" + k, v.shape, mybir.dt.from_np(v.dtype), kind="ExternalInput").ap()
           for k, v in arrays.items()}
    out = nc.dram_tensor("out", (N, D), F32, kind="ExternalOutput").ap()
    gat_layer(nc, out=out, **aps)
    r = run_bass_kernel_spmd(nc, [{"in_" + k: v for k, v in arrays.items()}], core_ids=[0])
    return r.results[0]["out"]
```

```python
from contextlib import ExitStack

import numpy as np

import concourse.bass as bass
from concourse import mybir

ALU = mybir.AluOpType
ACT = mybir.ActivationFunctionType
AX_X = mybir.AxisListType.X
RMAX = bass.bass_isa.ReduceOp.max
F32 = mybir.dt.float32
F32R = mybir.dt.float32r
BF16 = mybir.dt.bfloat16
I32 = mybir.dt.int32

P = 128
N = 8192
D = 512
F = D // 8
HID = 2 * D
SLOPE = 0.2
EPS = 1e-5
KT = D // P
HT = HID // P
NT = N // P
BLK = 512
NB = N // BLK
TB = BLK // P
PAIR = 2
NQ = NT // PAIR
RA = 4
RM = 2
SUB = 256
NS = BLK // SUB
TS = SUB // P

GROUP_CHAIN = 2
EPI_CHAIN = 6
MLP_CHAIN = 2


FC1_AT = (0, 1, 3, 4, 5, 7, 8, 9)
GELU_AT = tuple(c + 2 for c in FC1_AT)
SPLIT_AT = tuple(c + 3 for c in FC1_AT)
FC2_AT = tuple(c + 4 for c in FC1_AT)
FC_AT = (5, 7)
X2_AT = (7, 9)
XN_AT = (8, 11)
XT_AT = (9, 12)
HI_AT = (11, 14)
LO_AT = (12, 15)
Y_AT = 15
STORE_AT = 5
LOAD_AT = 6
BIAS_AT = 6
HALF = NQ // NS


def gat_layer(nc, x, adj_tiles, w, a, fc_wt, fc_b, ln1_g, ln1_b, ln2_g, ln2_b,
              fc1_wt, fc1_b, fc2_wt, fc2_b, ident_in, out):
    ctx = ExitStack()
    with ctx:
        def sb(name, shape, dt):
            return ctx.enter_context(nc.sbuf_tensor(name, shape, dt))

        def bank(name):
            return ctx.enter_context(nc.psum_tensor(name, [P, 512], F32))

        def sem(name):
            return ctx.enter_context(nc.semaphore(name))

        wpos = sb("wpos", [P, NT, 2 * F], F32R)
        wneg = sb("wneg", [P, NT, 2 * F], F32R)
        fc1_hi = sb("fc1_hi", [P, KT, HID], F32R)
        fc1_lo = sb("fc1_lo", [P, KT, HID], F32R)
        fc2_hi = sb("fc2_hi", [P, HT, D], F32R)
        fc2_lo = sb("fc2_lo", [P, HT, D], F32R)
        mpos = sb("mpos", [P, RM, PAIR * BLK], F32R)
        mneg = sb("mneg", [P, RM, PAIR * BLK], F32R)
        h2_hi = sb("h2_hi", [P, KT, SUB], F32R)
        h2_lo = sb("h2_lo", [P, KT, SUB], F32R)
        m_hi = sb("m_hi", [P, 2, SUB], F32R)
        m_lo = sb("m_lo", [P, 2, SUB], F32R)
        fcw2 = sb("fcw2", [P, D], F32)
        ident = sb("ident", [P, P], F32)
        ones = sb("ones", [P, P], F32)
        negd = sb("negd", [P, NT], F32)
        den_pos = sb("den_pos", [P, NT, 3], BF16)
        den_neg = sb("den_neg", [P, NT, 3], BF16)
        mean_wh = sb("mean_wh", [P, 1], F32)
        fc1_bias = sb("fc1_bias", [P, HT], F32)
        stats = sb("stats", [P, TB, 6], F32)
        mv = sb("mv", [P, TB, 2], F32)
        var_eps = sb("var_eps", [P, TB], F32)
        minus_half = sb("minus_half", [P, TB], F32)
        rstd = sb("rstd", [P, TB], F32)

        KIB = 256
        arena = sb("arena", [P, 46 * KIB], F32)

        def part(start, kib):
            return arena[:, start * KIB:(start + kib) * KIB]

        stage1 = part(0, 16).rearrange("p (k n) -> p k n", k=KT)
        stage2 = part(16, 16).rearrange("p (k n) -> p k n", k=HT)
        xin = [part(8 * i, 8).rearrange("p (t n) -> p t n", t=TB) for i in range(2)]
        ht = part(16, 8).rearrange("p (k n) -> p k n", k=KT)
        wht = part(24, 2)
        wh_all = part(26, 16).rearrange("p (t f) -> p t f", t=NT)
        full = part(0, 16).rearrange("p (t f) -> p t f", t=NT)
        sact = part(16, 2)[0:NT, 0:3 * P].rearrange("p (c n) -> p c n", c=3)
        adj_ring = part(0, 16).bitcast(I32).rearrange("p (r n) -> p r n", r=RA)
        sign_ring = part(16, 4).bitcast(BF16).rearrange("p (r n) -> p r n", r=RM)
        s_bc = part(20, 4).rearrange("p (r n) -> p r n", r=2)
        a_bc = part(24, 2)
        c_bc = part(26, 2)
        comb = part(28, 2)
        x2 = [part(30 + 4 * i, 4).rearrange("p (t n) -> p t n", t=TS) for i in range(2)]
        xn = part(38, 2)
        tmp = xn
        gl = part(40, 2).rearrange("p (r n) -> p r n", r=2)
        fcb_bc = part(42, 2)
        tail3 = part(40, 1).bitcast(BF16)[0:3, :]
        bias3 = part(44, 1).bitcast(BF16)
        ones3 = part(45, 1).bitcast(BF16)[:, 0:P]

        small = part(42, 4)
        wsb = small[:, 0:KT * F].rearrange("p (k f) -> p k f", k=KT)
        a2 = sb("a2", [F, 2], F32)
        g1 = sb("g1", [P, KT], F32)
        b1 = sb("b1", [P, KT], F32)
        g2 = sb("g2", [P, KT], F32)
        b2 = sb("b2", [P, KT], F32)
        fc1b = sb("fc1b", [P, HT], F32)
        small = small[:, KT * F:].rearrange("p (a n) -> p a n", n=NT)
        sd = small[:, 0:2, :]
        sac = small[:, 2:5, :]
        cols = small[:, 5:9, :]
        bd = small[:, 9:11, :]
        dmax = sb("dmax", [P, 2], F32)
        warm = sb("warm", [P, 2], F32)
        no_nb = sb("no_nb", [P, TB], F32)
        den1 = sb("den1", [P, TB], F32)
        rden = sb("rden", [P, TB], F32)

        sac_dram = nc.dram_tensor("sac_dram", (3, N), F32, kind="Internal").ap()

        banks = [bank(f"bank{i}") for i in range(8)]
        ps_t = banks[0:4]
        ps_wht, ps_whj, ps_sd, ps_misc = banks[4:8]
        ps_pos, ps_neg, ps_den, ps_x = banks[0:4]
        ps_f = banks[4:6]
        ps_y = banks[6:8]

        consts_in = sem("consts_in")
        stage_in = [sem("stage1_in"), sem("stage2_in")]
        rows_in = sem("rows_in")
        carrier = sem("carrier")
        consts_set = sem("consts_set")
        prep_chain = sem("prep_chain")
        bias_mm = sem("bias_mm")
        prep_done = sem("prep_done")
        xin_in = [sem("xin_in0"), sem("xin_in1")]
        xin_free = sem("xin_free")
        group_chain = sem("group_chain")
        var1 = sem("var1")
        rstd1 = sem("rstd1")
        xn1 = sem("xn1")
        xt1 = sem("xt1")
        h1 = sem("h1")
        wht_ps = sem("wht_ps")
        wht_sb = sem("wht_sb")
        whj_ps = sem("whj_ps")
        whj_sb = sem("whj_sb")
        dmax_part = sem("dmax_part")
        dmax_all = sem("dmax_all")
        cols_set = sem("cols_set")
        exps_set = sem("exps_set")
        sact_ps = sem("sact_ps")
        sact_sb = sem("sact_sb")
        sac_out = sem("sac_out")
        mean_ps = sem("mean_ps")
        split_chain = sem("split_chain")
        phase1_done = sem("phase1_done")

        adj_in = [sem(f"adj_in{i}") for i in range(RA)]
        adj_free = sem("adj_free")
        s_in = [sem("s_in0"), sem("s_in1")]
        s_free = sem("s_free")
        ac_in = sem("ac_in")
        ac_free = sem("ac_free")
        sign_made = sem("sign_made")
        signed = sem("signed")
        masks = sem("masks")
        masks_free = sem("masks_free")
        attn_ps = sem("attn_ps")
        attn_ps_free = sem("attn_ps_free")
        epi_chain = sem("epi_chain")
        den_parts = sem("den_parts")
        den_sum = sem("den_sum")
        den_read = sem("den_read")
        comb_made = sem("comb_made")
        comb_free = sem("comb_free")
        x_in = [sem("x_in0"), sem("x_in1")]
        xb_made = sem("xb_made")
        bias_chain = sem("bias_chain")
        bias3_made = sem("bias3_made")
        den_col = sem("den_col")
        den_col_read = sem("den_col_read")
        fc_ps = sem("fc_ps")
        x2_made = sem("x2_made")
        mlp_chain = sem("mlp_chain")
        var2 = sem("var2")
        rstd2 = sem("rstd2")
        xn2 = sem("xn2")
        xt2 = sem("xt2")
        h2hi_made = sem("h2hi_made")
        h2_made = sem("h2_made")
        f_ps = sem("f_ps")
        gelu_made = sem("gelu_made")
        mhi_made = sem("mhi_made")
        m_made = sem("m_made")
        m_free = sem("m_free")
        y_ps = sem("y_ps")
        y_made = sem("y_made")
        out_done = [sem("out_done0"), sem("out_done1")]

        block = ctx.enter_context(nc.Block())

        CONSTS = 10

        def has_store(ib, half):
            return not isinstance(ib, int) or 0 <= 2 * ib - 4 + half < 2 * NB - 2

        def blocks(eng, emit):
            emit(0, 0, True, ((False, False), (False, False)))
            emit(1, 1, True, ((False, True), (True, True)))
            with eng.Fori(1, NB // 2) as bi:
                emit(bi * 2, 0, True, ((True, True), (True, True)))
                emit(bi * 2 + 1, 1, True, ((True, True), (True, True)))
            emit(NB, 0, False, ((True, True), (True, True)))
            emit(NB + 1, 1, False, ((True, False), (False, False)))

        @block.sync
        def _(sp):
            sp.dma_start(stage1, fc1_wt.rearrange("(k p) n -> p k n", p=P)).then_inc(stage_in[0], 16)
            sp.dma_start(stage2, fc2_wt.rearrange("(k p) n -> p k n", p=P)).then_inc(stage_in[1], 16)
            for dst, src in ((ident[:, :], ident_in),
                             (wsb, w.rearrange("(k p) n -> p k n", p=P)),
                             (a2[:, :], a),
                             (g1[:, :], ln1_g), (b1[:, :], ln1_b), (g2[:, :], ln2_g), (b2[:, :], ln2_b),
                             (fc1b[:, :], fc1_b),
                             (fcw2[0:F, :], fc_wt), (fcw2[F:P, :], fc_wt)):
                sp.dma_start(dst, src).then_inc(consts_in, 16)

            xg = x.rearrange("(g t p) n -> g p t n", t=TB, p=P)
            sp.wait_ge(prep_done, 1)
            with sp.Fori(0, NB // 2) as gi:
                for par in range(2):
                    g = gi * 2 + par
                    sp.wait_ge(xin_free, g + 1)
                    sp.dma_start(xin[par], xg[bass.ds(g, 1)].rearrange("g p t n -> (g p) t n")
                                 ).then_inc(xin_in[par], 16)

            sp.wait_ge(sact_sb, 3)
            for c in range(3):
                sp.dma_start(sac_dram[c].rearrange("(t p) -> t p", p=P), sact[:, c, :]).then_inc(sac_out, 16)
            sp.wait_ge(sac_out, 48)
            sp.wait_ge(phase1_done, 1)
            sp.dma_start(fcb_bc, fc_b.broadcast_to([P, D])).then_inc(rows_in, 16)
            sp.dma_start(xn[0:3, :], fc2_b.broadcast_to([3, D])).then_inc(rows_in, 16)
            sp.dma_start(s_bc[:, 0, :], sac_dram[0:1, 0:BLK].broadcast_to([P, BLK])).then_inc(s_in[0], 16)

            xs = x.rearrange("(n t p) d -> n p t d", t=TS, p=P)
            os_ = out.rearrange("(n t p) d -> n p t d", t=TS, p=P)

            def block_sp(ib, par, attn, steps):
                for q in range(NQ):
                    half, c = divmod(q, HALF)
                    back, front = steps[half]
                    n = 2 * ib - 3 + half
                    if attn:
                        sp.wait_ge(adj_free, ib * NQ + (q + 1))
                        sp.dma_start(adj_ring[:, q % RA, :],
                                     adj_tiles[bass.ds(ib, 1), q].rearrange("b p n -> (b p) n")
                                     ).then_inc(adj_in[q % RA], 16)
                    if attn and q == 3 * HALF // 4:
                        sp.wait_ge(ac_free, ib + 1)
                        for k, dst in ((1, a_bc), (2, c_bc)):
                            sp.dma_start(dst, sac_dram[k:k + 1, bass.ds(ib * BLK, BLK)]
                                         .broadcast_to([P, BLK])).then_inc(ac_in, 16)
                        sp.wait_ge(s_free, ib + 1)
                        nxt = (ib + 1) % NB
                        sp.dma_start(s_bc[:, 1 - par, :], sac_dram[0:1, bass.ds(nxt * BLK, BLK)]
                                     .broadcast_to([P, BLK])).then_inc(s_in[1 - par], 16)
                    odd = half % 2
                    if c == STORE_AT and has_store(ib, half):
                        sp.wait_ge(y_made, n * TS + TS)
                        sp.sem_inc(carrier, 1)
                        sp.dma_start(os_[bass.ds(n - 1, 1)].rearrange("n p t d -> (n p) t d"), x2[odd]
                                     ).then_inc(out_done[odd], 16)
                    if c == LOAD_AT and front:
                        if has_store(ib, half):
                            sp.wait_ge(out_done[odd], (ib - 1) * 16)
                            sp.sem_inc(carrier, 1)
                        sp.dma_start(x2[odd], xs[bass.ds(n + 1, 1)].rearrange("n p t d -> (n p) t d")
                                     ).then_inc(x_in[odd], 16)

            blocks(sp, block_sp)
            for n in range(2 * NB - 2, 2 * NB):
                sp.wait_ge(y_made, n * TS + 2 * TS)
                sp.dma_start(os_[n], x2[n % 2]).then_inc(out_done[n % 2], 16)
            for odd in range(2):
                sp.wait_ge(out_done[odd], NB * 16)
            sp.wait_ge(s_in[0], (NB // 2 + 1) * 16)

        @block.gpsimd
        def _(pool):
            pool.memset(warm[:, :], 0.0).then_inc(consts_set, 1)
            pool.memset(ones[:, :], 1.0).then_inc(consts_set, 1)
            pool.memset(minus_half[:, :], -0.5).then_inc(consts_set, 1)
            pool.wait_ge(consts_set, 4)
            with pool.Fori(0, NB) as g:
                pool.wait_ge(var1, g + 1)
                pool.tensor_tensor(rstd[:, :], var_eps[:, :], minus_half[:, :], ALU.pow).then_inc(rstd1, 1)
            pool.wait_ge(dmax_part, 1)
            pool.partition_all_reduce(dmax[:, 1:2], dmax[:, 0:1], P, RMAX).then_inc(dmax_all, 1)

            pool.wait_ge(phase1_done, 1)
            pool.wait_ge(rows_in, 32)

            def block_pool(ib, par, attn, steps):
                for half in range(NS):
                    back, front = steps[half]
                    n = 2 * ib - 3 + half
                    odd = half % 2
                    for c in range(HALF):
                        if front and c == BIAS_AT:
                            pool.wait_ge(x_in[odd], ib * 16)
                            for t in range(TS):
                                pool.tensor_tensor(x2[odd][:, t, :], x2[odd][:, t, :], fcb_bc, ALU.add
                                                   ).then_inc(xb_made, 1)
                        for t in range(TS):
                            if front and c == X2_AT[t]:
                                pool.wait_ge(var2, n * TS + (TS + t + 1))
                                pool.tensor_tensor(rstd[:, t:t + 1], var_eps[:, t:t + 1],
                                                   minus_half[:, t:t + 1], ALU.pow).then_inc(rstd2, 1)
                        for h in range(HT):
                            if back and c == SPLIT_AT[h]:
                                pool.wait_ge(mhi_made, n * HT + (h + 1))
                                pool.tensor_tensor(m_lo[:, h % 2, :], gl[:, h % 2, :],
                                                   m_hi[:, h % 2, :].bitcast(F32), ALU.subtract
                                                   ).then_inc(m_made, 1)

            blocks(pool, block_pool)

        @block.scalar
        def _(act):
            act.sem_inc(masks, 2 * RM)
            act.sem_inc(whj_sb, 2)
            act.sem_inc(gelu_made, 2)
            act.wait_ge(consts_in, 16 * CONSTS)
            act.wait_ge(consts_set, 4)
            with act.Fori(0, NB) as g:
                for k in range(KT):
                    act.wait_ge(xt1, g * KT + (k + 1))
                    if k == 0:
                        act.wait_ge(wht_ps, g + 1)
                    act.activation(ht[:, k, :], ps_t[k][:, :], ACT.Identity, bias=b1[:, k:k + 1],
                                   scale=g1[:, k:k + 1]).then_inc(h1, 1)
                act.wait_ge(wht_ps, g + 2)
                act.copy(wht[0:F, :], ps_wht[0:F, :]).then_inc(wht_sb, 1)
                act.wait_ge(whj_ps, g + 1)
                act.copy(wh_all[:, bass.ds(g * TB, TB), :],
                         ps_whj[:, 0:TB * F].rearrange("p (t f) -> p t f", t=TB)).then_inc(whj_sb, 1)
                act.copy(sd[:, :, bass.ds(g * TB, TB)],
                         ps_sd[:, 0:2 * TB].rearrange("p (t c) -> p c t", c=2)).then_inc(whj_sb, 1)
            act.wait_ge(cols_set, 4)
            act.activation(bd[:, 0, :], cols[:, 0, :], ACT.Exp).then_inc(exps_set, 1)
            act.activation(bd[:, 1, :], cols[:, 0, :], ACT.Exp, scale=SLOPE).then_inc(exps_set, 1)
            act.activation(sac[:, 1, :], cols[:, 2, :], ACT.Exp, scale=1 - SLOPE).then_inc(exps_set, 1)
            act.activation(sac[:, 2, :], cols[:, 3, :], ACT.Exp, scale=SLOPE - 1).then_inc(exps_set, 1)
            act.copy(sac[:, 0, :], sd[:, 0, :]).then_inc(exps_set, 1)
            act.wait_ge(sact_ps, 1)
            for c in range(3):
                act.copy(sact[:, c, :], ps_misc[0:NT, c * P:(c + 1) * P]).then_inc(sact_sb, 1)

            act.wait_ge(phase1_done, 1)

            def block_act(ib, par, attn, steps):
                act.activation(warm[:, 1:2], warm[:, 0:1], ACT.Gelu)
                for q in range(NQ):
                    half, c = divmod(q, HALF)
                    back, front = steps[half]
                    n = 2 * ib - 3 + half
                    if attn:
                        act.wait_ge(signed, ib * NQ + (q + 1))
                        act.wait_ge(masks_free, ib * NQ + (q + 1))
                        src = sign_ring[:, q % RM, :]
                        act.activation(mpos[:, q % RM, :], src, ACT.Relu, scale=2.0).then_inc(masks, 1)
                        act.activation(mneg[:, q % RM, :], src, ACT.Relu, scale=-2.0).then_inc(masks, 1)
                    for h in range(HT):
                        if back and c == GELU_AT[h]:
                            act.wait_ge(f_ps, n * HT + (h + 2))
                            act.wait_ge(m_made, n * HT + (h + 1))
                            act.activation(gl[:, h % 2, :], ps_f[h % 2][:, 0:SUB], ACT.Gelu,
                                           bias=fc1_bias[:, h:h + 1]).then_inc(gelu_made, 1)
                    for t in range(TS):
                        if front and c == HI_AT[t]:
                            act.wait_ge(xt2, n * TS + (TS + t + 2))
                            if t == 0:
                                act.wait_ge(f_ps, n * HT + (HT + 1))
                            act.copy(h2_hi[:, :, t * P:(t + 1) * P],
                                     ps_x[:, :].rearrange("p (k n) -> p k n", k=KT)).then_inc(h2hi_made, 1)

            blocks(act, block_act)

        @block.vector
        def _(dve):
            dve.memset(mean_wh[:, :], 0.0).then_inc(consts_set, 1)
            dve.sem_inc(xin_free, 2)
            dve.sem_inc(adj_free, RA)
            dve.sem_inc(ac_free, 1)
            dve.sem_inc(s_free, 1)
            dve.sem_inc(m_made, 2)
            dve.sem_inc(attn_ps_free, 1)
            dve.sem_inc(y_made, TS)
            dve.sem_inc(h2_made, 1)

            dve.wait_ge(consts_in, 16 * CONSTS)
            dve.wait_ge(stage_in[0], 16)
            dve.wait_ge(bias_mm, 1)
            dve.tensor_tensor(fc1_bias[:, :], ps_misc[:, 0:HT], fc1b[:, :], ALU.add).then_inc(prep_chain, 1)
            for k in range(KT):
                dve.tensor_scalar(stage1[:, k, :], stage1[:, k, :], g2[:, k:k + 1], None, ALU.mult
                                  ).then_inc(prep_chain, 1)
            dve.wait_ge(prep_chain, 5)
            dve.tensor_copy(fc1_hi[:, :, :], stage1).then_inc(prep_chain, 1)
            dve.wait_ge(stage_in[1], 16)
            dve.tensor_copy(fc2_hi[:, :, :], stage2).then_inc(prep_chain, 1)
            dve.wait_ge(prep_chain, 7)
            dve.tensor_tensor(fc1_lo[:, :, :], stage1, fc1_hi[:, :, :].bitcast(F32), ALU.subtract
                              ).then_inc(prep_chain, 1)
            dve.tensor_tensor(fc2_lo[:, :, :], stage2, fc2_hi[:, :, :].bitcast(F32), ALU.subtract
                              ).then_inc(prep_chain, 1)
            dve.wait_ge(prep_chain, 9)
            dve.sem_inc(prep_done, 1)

            with dve.Fori(0, NB // 2) as gi:
                for par in range(2):
                    g = gi * 2 + par
                    base = g * GROUP_CHAIN
                    dve.wait_ge(xin_in[par], gi * 16 + 16)
                    for t in range(TB):
                        ins = dve.bn_stats(stats[:, t, :], xin[par][:, t, :])
                    ins.then_inc(group_chain, 1)
                    dve.wait_ge(group_chain, base + 1)
                    dve.sem_inc(carrier, 1)
                    for t in range(TB):
                        ins = dve.bn_aggr(mv[:, t, :], stats[:, t, :])
                    ins.then_inc(group_chain, 1)
                    dve.wait_ge(group_chain, base + 2)
                    dve.tensor_scalar(var_eps[:, :], mv[:, :, 1], EPS, None, ALU.add).then_inc(var1, 1)
                    dve.wait_ge(rstd1, g + 1)
                    for t in range(TB):
                        ins = dve.tensor_scalar(xin[par][:, t, :], xin[par][:, t, :], mv[:, t, 0:1],
                                                rstd[:, t:t + 1], ALU.subtract, ALU.mult)
                    ins.then_inc(xn1, 1)

            dve.wait_ge(whj_sb, 2 * NB + 2)
            dve.tensor_reduce(dmax[:, 0:1], sd[:, 1, :], AX_X, ALU.max).then_inc(dmax_part, 1)
            dve.tensor_scalar(negd[:, :], sd[:, 1, :], -1.0, None, ALU.mult).then_inc(split_chain, 1)
            dve.wait_ge(dmax_all, 1)
            dve.tensor_scalar(cols[:, 0, :], sd[:, 1, :], dmax[:, 1:2], None, ALU.subtract).then_inc(cols_set, 1)
            dve.tensor_scalar(cols[:, 1, :], sd[:, 0, :], dmax[:, 1:2], None, ALU.add).then_inc(cols_set, 1)
            dve.tensor_scalar(cols[:, 2, :], sd[:, 0, :], dmax[:, 1:2], 0.0, ALU.add, ALU.min).then_inc(cols_set, 1)
            dve.tensor_scalar(cols[:, 3, :], sd[:, 0, :], dmax[:, 1:2], 0.0, ALU.add, ALU.max).then_inc(cols_set, 1)
            dve.wait_ge(exps_set, 2)
            step = 1
            for c, wdst, ddst in ((0, wpos, den_pos), (1, wneg, den_neg)):
                fac = bd[:, c, :]
                dve.tensor_tensor(full, wh_all, fac.unsqueeze(2).broadcast_to([P, NT, F]), ALU.mult
                                  ).then_inc(split_chain, 1)
                dve.tensor_copy(ddst[:, :, 0], fac).then_inc(split_chain, 1)
                step += 2
                dve.wait_ge(split_chain, step)
                dve.tensor_copy(wdst[:, :, 0:F], full).then_inc(split_chain, 1)
                dve.wait_ge(exps_set, 5)
                dve.tensor_tensor(cols[:, 0, :], fac, ddst[:, :, 0], ALU.subtract).then_inc(split_chain, 1)
                step += 2
                dve.wait_ge(split_chain, step)
                dve.tensor_tensor(wdst[:, :, F:2 * F], full, wdst[:, :, 0:F].bitcast(F32), ALU.subtract
                                  ).then_inc(split_chain, 1)
                dve.tensor_copy(ddst[:, :, 1], cols[:, 0, :]).then_inc(split_chain, 1)
                step += 2
                dve.wait_ge(split_chain, step)
                dve.tensor_tensor(ddst[:, :, 2], cols[:, 0, :], ddst[:, :, 1], ALU.subtract).then_inc(split_chain, 1)
                step += 1
            dve.wait_ge(mean_ps, 1)
            dve.tensor_scalar(mean_wh[0:F, :], ps_wht[0:F, 0:1], 1.0 / N, None, ALU.mult).then_inc(split_chain, 1)
            dve.memset(ps_den[:, :], 0.0).then_inc(split_chain, 1)
            dve.wait_ge(split_chain, step + 2)
            dve.wait_ge(sac_out, 48)
            dve.sem_inc(phase1_done, 1)

            dve.wait_ge(rows_in, 32)
            dve.memset(ones3, 1.0).then_inc(bias_chain, 1)
            for p3 in range(3):
                dve.tensor_copy(tail3, xn[0:3, :]).then_inc(bias_chain, 1)
                dve.wait_ge(bias_chain, 1 + 3 * p3 + 1)
                if p3 == 0:
                    dve.tensor_scalar(bias3[0:3, :], tail3, ident[0:3, 0:1], None, ALU.mult).then_inc(bias_chain, 1)
                else:
                    dve.scalar_tensor_tensor(out=bias3[0:3, :], in0=tail3, scalar=ident[0:3, p3:p3 + 1],
                                             in1=bias3[0:3, :], op0=ALU.mult, op1=ALU.add).then_inc(bias_chain, 1)
                dve.tensor_tensor(xn[0:3, :], xn[0:3, :], tail3, ALU.subtract).then_inc(bias_chain, 1)
                dve.wait_ge(bias_chain, 1 + 3 * p3 + 3)
            dve.sem_inc(bias3_made, 1)

            def s_loads(ib, par):
                if isinstance(ib, int):
                    return (ib // 2 + 1) * 16
                return (ib - par) * 8 + 16

            def sign(ib, par, q):
                dve.wait_ge(masks, ib * (2 * NQ) + (2 * q + 2))
                for u in range(PAIR):
                    j = PAIR * q + u
                    ins = dve.tensor_scalar(sign_ring[:, q % RM, u * BLK:(u + 1) * BLK], s_bc[:, par, :],
                                            negd[:, j:j + 1], 0.5, ALU.is_ge, ALU.subtract)
                ins.then_inc(sign_made, 1)
                if q == NQ - 1:
                    dve.wait_ge(sign_made, ib * NQ + NQ)
                    dve.sem_inc(s_free, 1)

            def mask_sign(ib, q):
                k = ib * NQ + q
                dve.wait_ge(sign_made, k + 1)
                dve.wait_ge(adj_in[q % RA], ib * (16 * NQ // RA) + 16 * (q // RA + 1))
                dve.scalar_tensor_tensor(out=sign_ring[:, q % RM, :], in0=adj_ring[:, q % RA, :], scalar=0.0,
                                         in1=sign_ring[:, q % RM, :], op0=ALU.is_gt, op1=ALU.mult
                                         ).then_inc(signed, 1)
                dve.wait_ge(signed, k + 1)
                dve.sem_inc(adj_free, 1)

            def epilogue(ib, q):
                e = ib * EPI_CHAIN
                if q == 0:
                    dve.wait_ge(attn_ps, ib + 1)
                    dve.wait_ge(ac_in, ib * 32 + 32)
                    dve.wait_ge(comb_free, ib + 1)
                    dve.tensor_tensor(comb, a_bc, ps_pos[:, :], ALU.mult).then_inc(epi_chain, 1)
                    dve.tensor_tensor(tmp, c_bc, ps_neg[:, :], ALU.mult).then_inc(epi_chain, 1)
                    dve.wait_ge(epi_chain, e + 1)
                    h = P // 2
                    dve.tensor_tensor(a_bc[0:h, :], a_bc[0:h, :], ps_den[0:h, :], ALU.mult).then_inc(den_parts, 1)
                    dve.tensor_tensor(a_bc[h:P, :], c_bc[h:P, :], ps_den[h:P, :], ALU.mult).then_inc(den_parts, 1)
                if q == 1:
                    dve.wait_ge(den_parts, ib * 2 + 2)
                    dve.sem_inc(attn_ps_free, 1)
                    dve.wait_ge(epi_chain, e + 2)
                    dve.tensor_tensor(comb, comb, tmp, ALU.add).then_inc(epi_chain, 1)
                if q == 3:
                    dve.wait_ge(den_col, ib + 1)
                    dve.tensor_scalar(no_nb[:, :], ps_x[:, 0:TB], 0.0, None, ALU.is_equal).then_inc(epi_chain, 1)
                    dve.wait_ge(epi_chain, e + 4)
                    dve.tensor_tensor(den1[:, :], no_nb[:, :], ps_x[:, 0:TB], ALU.add).then_inc(epi_chain, 1)
                    dve.wait_ge(epi_chain, e + 5)
                    dve.sem_inc(den_col_read, 1)
                    dve.reciprocal(rden[:, :], den1[:, :]).then_inc(epi_chain, 1)
                if q == 5:
                    dve.wait_ge(den_sum, ib + 1)
                    dve.tensor_scalar(c_bc, ps_x[:, :], 0.0, None, ALU.is_equal).then_inc(den_read, 1)
                    dve.wait_ge(den_read, ib + 1)
                    dve.wait_ge(epi_chain, e + 6)
                    dve.scalar_tensor_tensor(out=comb, in0=c_bc, scalar=mean_wh[:, 0:1], in1=comb,
                                             op0=ALU.mult, op1=ALU.add).then_inc(comb_made, 1)
                    dve.wait_ge(comb_made, ib + 1)
                    dve.sem_inc(ac_free, 1)

            def rows_and_stats(n, half, t):
                slot, tile = x2[half][:, t, :], TS * half + t
                c = n * (TS * MLP_CHAIN) + t * MLP_CHAIN
                dve.wait_ge(xb_made, n * TS + (t + 1))
                dve.wait_ge(fc_ps, n * TS + (t + 1))
                dve.scalar_tensor_tensor(out=slot, in0=ps_x[:, :], scalar=rden[:, tile:tile + 1], in1=slot,
                                         op0=ALU.mult, op1=ALU.add).then_inc(x2_made, 1)
                dve.wait_ge(x2_made, n * TS + (t + 1))
                dve.bn_stats(stats[:, t, :], slot).then_inc(mlp_chain, 1)
                dve.wait_ge(mlp_chain, c + 1)
                dve.sem_inc(carrier, 1)
                dve.bn_aggr(mv[:, t, :], stats[:, t, :]).then_inc(mlp_chain, 1)
                dve.wait_ge(mlp_chain, c + 2)
                dve.tensor_scalar(var_eps[:, t:t + 1], mv[:, t, 1:2], EPS, None, ALU.add).then_inc(var2, 1)

            def normalise(n, half, t):
                dve.wait_ge(rstd2, n * TS + (t + 1))
                dve.wait_ge(xt2, n * TS + (t + 1))
                dve.tensor_scalar(xn, x2[half][:, t, :], mv[:, t, 0:1], rstd[:, t:t + 1],
                                  ALU.subtract, ALU.mult).then_inc(xn2, 1)

            def low_half(n, t):
                dve.wait_ge(h2hi_made, n * TS + (t + 1))
                cut = slice(t * P, (t + 1) * P)
                dve.tensor_tensor(h2_lo[:, :, cut], ps_x[:, :].rearrange("p (k n) -> p k n", k=KT),
                                  h2_hi[:, :, cut].bitcast(F32), ALU.subtract).then_inc(h2_made, 1)

            def gelu_high(n, h):
                dve.wait_ge(gelu_made, n * HT + (h + 3))
                dve.wait_ge(m_free, n * HT + (h + 1))
                dve.tensor_copy(m_hi[:, h % 2, :], gl[:, h % 2, :]).then_inc(mhi_made, 1)

            def finish_rows(n, half):
                dve.wait_ge(y_ps, n + 1)
                for t in range(TS):
                    slot = x2[1 - half][:, t, :]
                    dve.tensor_tensor(slot, ps_y[t][:, :], slot, ALU.add).then_inc(y_made, 1)

            def block_dve(ib, par, attn, steps):
                if attn:
                    dve.wait_ge(s_in[par], s_loads(ib, par))
                    sign(ib, par, 0)
                for q in range(NQ):
                    half, c = divmod(q, HALF)
                    back, front = steps[half]
                    n = 2 * ib - 3 + half
                    if attn:
                        mask_sign(ib, q)
                        if q + 1 < NQ:
                            sign(ib, par, q + 1)
                    if steps[0][1]:
                        epilogue(ib - 1, q)
                    for h in range(HT):
                        if back and c == SPLIT_AT[h]:
                            gelu_high(n, h)
                    for t in range(TS):
                        if front and c == LO_AT[t]:
                            low_half(n + 1, t)
                        if front and c == X2_AT[t]:
                            rows_and_stats(n + 1, half, t)
                        if front and c == XN_AT[t]:
                            normalise(n + 1, half, t)
                    if back and c == Y_AT:
                        finish_rows(n, half)

            blocks(dve, block_dve)

        @block.tensor
        def _(pe):
            pe.sem_inc(wht_ps, 1)
            pe.sem_inc(masks_free, RM)
            pe.sem_inc(f_ps, 1)
            pe.sem_inc(m_free, 2)
            pe.sem_inc(comb_free, 1)
            pe.sem_inc(xt2, 1)
            pe.wait_ge(consts_in, 16 * CONSTS)
            pe.wait_ge(stage_in[0], 16)
            for h in range(HT):
                for k in range(KT):
                    ins = pe.matmul(ps_misc[:, h:h + 1], stage1[:, k, h * P:(h + 1) * P], b2[:, k:k + 1],
                                    start=(k == 0), stop=(k == KT - 1))
            ins.then_inc(bias_mm, 1)

            with pe.Fori(0, NB // 2) as gi:
                for par in range(2):
                    g = gi * 2 + par
                    pe.wait_ge(xn1, g + 1)
                    for k in range(KT):
                        for t in range(TB):
                            ins = pe.transpose(ps_t[k][:, t * P:(t + 1) * P], xin[par][:, t, k * P:(k + 1) * P],
                                               ident[:, :])
                        ins.then_inc(xt1, 1)
                    pe.wait_ge(xt1, g * KT + KT)
                    pe.sem_inc(xin_free, 1)
                    for k in range(KT):
                        pe.wait_ge(h1, g * KT + (k + 1))
                        ins = pe.matmul(ps_wht[0:F, :], wsb[:, k, :], ht[:, k, :], start=(k == 0), stop=(k == KT - 1))
                    ins.then_inc(wht_ps, 1)
                    pe.wait_ge(wht_sb, g + 1)
                    pe.wait_ge(whj_sb, g * 2 + 2)
                    for t in range(TB):
                        pe.matmul(ps_sd[:, 2 * t:2 * t + 2], wht[0:F, t * P:(t + 1) * P], a2[:, :],
                                  start=True, stop=True)
                        ins = pe.transpose(ps_whj[:, t * F:(t + 1) * F], wht[0:F, t * P:(t + 1) * P],
                                           ident[0:F, 0:F])
                    ins.then_inc(whj_ps, 1)

            pe.wait_ge(exps_set, 5)
            for c in range(3):
                ins = pe.transpose(ps_misc[0:NT, c * P:(c + 1) * P], sac[:, c, :], ident[:, :])
            ins.then_inc(sact_ps, 1)
            pe.wait_ge(consts_set, 4)
            for t in range(NT):
                ins = pe.matmul(ps_wht[0:F, 0:1], wh_all[:, t, :], ones[:, 0:1], start=(t == 0), stop=(t == NT - 1))
            ins.then_inc(mean_ps, 1)

            def attention(ib, q):
                pe.wait_ge(masks, ib * (2 * NQ) + (2 * q + 6))
                if q == 0:
                    pe.wait_ge(attn_ps_free, ib + 1)
                r = q % RM
                for u in range(PAIR):
                    j = PAIR * q + u
                    cut = slice(u * BLK, (u + 1) * BLK)
                    pe.matmul(ps_pos[:, :], wpos[:, j, :], mpos[:, r, cut], start=(j == 0), stop=(j == NT - 1))
                    pe.matmul(ps_neg[:, :], wneg[:, j, :], mneg[:, r, cut], start=(j == 0), stop=(j == NT - 1))
                for c, (m, dw) in enumerate(((mpos, den_pos), (mneg, den_neg))):
                    for u in range(PAIR):
                        j = PAIR * q + u
                        o = 32 * (2 * c + u)
                        half = m[:, r, u * BLK:(u + 1) * BLK].bitcast(BF16)[:, 1::2]
                        ins = pe.matmul(ps_den[o:o + 3, :], dw[:, j, :], half, start=(q == 0), stop=(q == NQ - 1),
                                        tile_position=(0, o))
                ins.then_inc(masks_free, 1)
                if q == NQ - 1:
                    pe.wait_ge(masks_free, ib * NQ + (NQ + RM))
                    pe.sem_inc(attn_ps, 1)

            def denominators(ib, q):
                if q == 1:
                    pe.wait_ge(den_parts, ib * 2 + 2)
                    for t in range(TB):
                        ins = pe.matmul(ps_x[:, t:t + 1], a_bc[:, t * P:(t + 1) * P], ones[:, 0:1],
                                        start=True, stop=True)
                    ins.then_inc(den_col, 1)
                if q == 3:
                    pe.wait_ge(den_col_read, ib + 1)
                    pe.matmul(ps_x[:, :], ones[:, :], a_bc, start=True, stop=True).then_inc(den_sum, 1)

            def fc(ib, n, half, t):
                pe.wait_ge(comb_made, ib + 1)
                if t > 0:
                    pe.wait_ge(x2_made, n * TS + t)
                c = (half * TS + t) * P
                pe.matmul(ps_x[:, :], comb[:, c:c + P], fcw2[:, :], start=True, stop=True).then_inc(fc_ps, 1)
                if half == NS - 1 and t == TS - 1:
                    pe.wait_ge(fc_ps, n * TS + TS)
                    pe.sem_inc(comb_free, 1)

            def transpose_rows(n, t):
                pe.wait_ge(xn2, n * TS + (t + 1))
                if t == 0:
                    pe.wait_ge(x2_made, n * TS + TS)
                pe.wait_ge(h2_made, n * TS + (t + 1))
                for k in range(KT):
                    ins = pe.transpose(ps_x[:, k * P:(k + 1) * P], xn[:, k * P:(k + 1) * P], ident[:, :])
                ins.then_inc(xt2, 1)

            def fc1(n, h):
                if h == 0:
                    pe.wait_ge(h2_made, n * TS + (TS + 1))
                pe.wait_ge(gelu_made, n * HT + (h + 1))
                cut = slice(h * P, (h + 1) * P)
                i = 0
                for wt, v in ((fc1_hi, h2_hi), (fc1_lo, h2_hi), (fc1_hi, h2_lo)):
                    for k in range(KT):
                        ins = pe.matmul(ps_f[h % 2][:, 0:SUB], wt[:, k, cut], v[:, k, :],
                                        start=(i == 0), stop=(i == 3 * KT - 1))
                        i += 1
                ins.then_inc(f_ps, 1)

            def fc2(n, h):
                if h == 0:
                    pe.wait_ge(y_made, n * TS + TS)
                    for t in range(TS):
                        pe.matmul(ps_y[t][:, :], ones3[0:3, :], bias3[0:3, :], start=True, stop=False)
                pe.wait_ge(m_made, n * HT + (h + 3))
                for t in range(TS):
                    cut = slice(t * P, (t + 1) * P)
                    for i, (m, wt) in enumerate(((m_hi, fc2_hi), (m_hi, fc2_lo), (m_lo, fc2_hi))):
                        ins = pe.matmul(ps_y[t][:, :], m[:, h % 2, cut], wt[:, h, :],
                                        start=False, stop=(h == HT - 1 and i == 2))
                ins.then_inc(m_free, 1)
                if h == HT - 1:
                    pe.wait_ge(m_free, n * HT + (HT + 2))
                    pe.sem_inc(y_ps, 1)

            pe.wait_ge(phase1_done, 1)
            pe.wait_ge(bias3_made, 1)

            def block_pe(ib, par, attn, steps):
                for q in range(NQ):
                    half, c = divmod(q, HALF)
                    back, front = steps[half]
                    n = 2 * ib - 3 + half
                    for h in range(HT):
                        if back and c == FC2_AT[h]:
                            fc2(n, h)
                        if back and c == FC1_AT[h]:
                            fc1(n, h)
                    if steps[0][1]:
                        denominators(ib - 1, q)
                    for t in range(TS):
                        if front and c == XT_AT[t]:
                            transpose_rows(n + 1, t)
                        if front and c == FC_AT[t]:
                            fc(ib - 1, n + 1, half, t)
                    if attn:
                        attention(ib, q)

            blocks(pe, block_pe)


def kernel(**inputs):
    import concourse.bacc as bacc
    from concourse.bass_utils import run_bass_kernel_spmd

    nc = bacc.Bacc("TRN2", target_bir_lowering=False, num_devices=1)
    g = {k.replace("L0_gnn_", ""): np.asarray(v) for k, v in inputs.items()}
    adj = g["adj"].reshape(NB, BLK, NQ, PAIR, P).transpose(0, 2, 4, 3, 1).reshape(NB, NQ, P, PAIR * BLK)

    def columns(v):
        return v.reshape(-1, P).T

    arrays = {
        "x": g["x"], "adj_tiles": adj, "w": g["W"], "a": g["a"].reshape(2, F).T,
        "fc_wt": g["fc_w"].T, "fc_b": g["fc_b"].reshape(1, D),
        "ln1_g": columns(g["ln1_g"]), "ln1_b": columns(g["ln1_b"]),
        "ln2_g": columns(g["ln2_g"]), "ln2_b": columns(g["ln2_b"]),
        "fc1_wt": g["fc1_w"].T, "fc1_b": columns(g["fc1_b"]),
        "fc2_wt": g["fc2_w"].T, "fc2_b": g["fc2_b"].reshape(1, D),
        "ident_in": np.eye(P, dtype=np.float32),
    }
    arrays = {k: np.ascontiguousarray(v) for k, v in arrays.items()}
    aps = {k: nc.dram_tensor("in_" + k, v.shape, mybir.dt.from_np(v.dtype), kind="ExternalInput").ap()
           for k, v in arrays.items()}
    out = nc.dram_tensor("out", (N, D), F32, kind="ExternalOutput").ap()
    gat_layer(nc, out=out, **aps)
    r = run_bass_kernel_spmd(nc, [{"in_" + k: v for k, v in arrays.items()}], core_ids=[0])
    return r.results[0]["out"]
```

```python
from contextlib import ExitStack

import numpy as np

import concourse.bass as bass
from concourse import mybir

ALU = mybir.AluOpType
ACT = mybir.ActivationFunctionType
AX_X = mybir.AxisListType.X
F32 = mybir.dt.float32
F32R = mybir.dt.float32r
BF16 = mybir.dt.bfloat16
I32 = mybir.dt.int32

P = 128
N = 8192
D = 512
F = D // 8
FE = F + 2
HID = 2 * D
SLOPE = 0.2
EPS = 1e-5
KT = D // P
HT = HID // P
NT = N // P
BLK = 512
NB = N // BLK
TB = BLK // P
PAIR = 2
NQ = NT // PAIR
RA = 4
RM = 2
RX = 4
SUB = 256
NS = BLK // SUB
TS = SUB // P

GROUP_CHAIN = 2
EPI_CHAIN = 6
MLP_CHAIN = 2

FC1_AT = (0, 0, 2, 3, 7, 8, 8, 10)
GELU_AT = (0, 1, 5, 6, 7, 10, 11, 12)
SPLIT_AT = (2, 4, 5, 5, 8, 12, 12, 12)
FC2_AT = (1, 4, 6, 7, 10, 11, 13, 14)
FC_AT = (5, 9)
X2_AT = (8, 11)
XN_AT = (10, 12)
XT_AT = (10, 12)
HI_AT = (11, 14)
LO_AT = (12, 15)
Y_AT = 15
STORE_AT = 5
LOAD_AT = 6
BIAS_AT = 6
HALF = NQ // NS
WT = NT // 4
WEIGHTS_AT = (0, 1, 3, 5)
STAGE1_AT = 10
FC1_PREP_AT = 10
BIAS_MM_AT = 10
ROW3_AT = 14
BIAS3_AT = 16
STAGE2_AT = 21
FC2_PREP_AT = 22
FCB_AT = 30


def gat_layer(nc, x, adj_tiles, w, w_t, a, fc_wt, fc_b, ln1_g, ln1_b, ln2_g, ln2_b,
              fc1_wt, fc1_b, fc2_wt, fc2_b, ident_in, out):
    ctx = ExitStack()
    with ctx:
        def sb(name, shape, dt):
            return ctx.enter_context(nc.sbuf_tensor(name, shape, dt))

        def bank(name):
            return ctx.enter_context(nc.psum_tensor(name, [P, 512], F32))

        def sem(name):
            return ctx.enter_context(nc.semaphore(name))

        def early(names, shape):
            with ExitStack() as own:
                return [own.enter_context(nc.sbuf_tensor(name, shape, F32))[:, :, :] for name in names]

        xin = early([f"xin{i}" for i in range(RX)], [P, TB, D])
        wpos = sb("wpos", [P, NT, 2 * F], F32R)
        wneg = sb("wneg", [P, NT, 2 * F], F32R)
        full = early(["full_pos", "full_neg"], [P, NT, F])
        fc1_hi = sb("fc1_hi", [P, KT, HID], F32R)
        fc1_lo = sb("fc1_lo", [P, KT, HID], F32R)
        fc2_hi = sb("fc2_hi", [P, HT, D], F32R)
        fc2_lo = sb("fc2_lo", [P, HT, D], F32R)
        mpos = sb("mpos", [P, RM, PAIR * BLK], F32R)
        mneg = sb("mneg", [P, RM, PAIR * BLK], F32R)
        h2_hi = sb("h2_hi", [P, KT, SUB], F32R)
        h2_lo = sb("h2_lo", [P, KT, SUB], F32R)
        m_hi = sb("m_hi", [P, 2, SUB], F32R)
        m_lo = sb("m_lo", [P, 2, SUB], F32R)
        fcw2 = sb("fcw2", [P, D], F32)
        ident = sb("ident", [P, P], F32)
        ones = sb("ones", [P, P], F32)
        negd = sb("negd", [P, NT], F32)
        den_pos = sb("den_pos", [P, NT, 3], BF16)
        den_neg = sb("den_neg", [P, NT, 3], BF16)
        mean_wh = sb("mean_wh", [P, 1], F32)
        fc1_bias = sb("fc1_bias", [P, HT], F32)
        stats_2 = sb("stats_2", [P, 2, TB, 6], F32)
        mv_2 = sb("mv_2", [P, 2, TB, 2], F32)
        rstd_2 = sb("rstd_2", [P, 2, TB], F32)
        stats, mv, rstd = stats_2[:, 0], mv_2[:, 0], rstd_2[:, 0]
        var_eps = sb("var_eps", [P, TB], F32)
        minus_half = sb("minus_half", [P, TB], F32)

        KIB = 256
        arena = sb("arena", [P, 46 * KIB], F32)

        def part(start, kib):
            return arena[:, start * KIB:(start + kib) * KIB]

        stage = part(28, 16)
        stage1 = stage.rearrange("p (k n) -> p k n", k=KT)
        stage2 = stage.rearrange("p (k n) -> p k n", k=HT)
        ht = part(16, 8).rearrange("p (k n) -> p k n", k=KT)
        w_rows = part(24, 2)[0:F, :]
        wh_all = part(26, 16).rearrange("p (t f) -> p t f", t=NT)
        sact = part(24, 2)[0:NT, 0:3 * P].rearrange("p (c n) -> p c n", c=3)
        adj_ring = part(0, 16).bitcast(I32).rearrange("p (r n) -> p r n", r=RA)
        sign_ring = part(16, 4).bitcast(BF16).rearrange("p (r n) -> p r n", r=RM)
        s_bc = part(20, 4).rearrange("p (r n) -> p r n", r=2)
        a_bc = part(24, 2)
        c_bc = part(26, 2)
        comb = part(28, 2)
        x2 = [part(30 + 4 * i, 4).rearrange("p (t n) -> p t n", t=TS) for i in range(2)]
        xn = part(38, 2)
        tmp = xn
        gl = part(40, 2).rearrange("p (r n) -> p r n", r=2)
        fcb_bc = part(42, 2)
        row3 = c_bc[0:3, :]
        tail3 = part(24, 1).bitcast(BF16)[0:3, :]
        bias3 = part(44, 1).bitcast(BF16)
        ones3 = part(45, 1).bitcast(BF16)[:, 0:P]

        small = part(42, 4)
        wsb = small[:, 0:KT * FE].rearrange("p (k f) -> p k f", k=KT)
        a2 = sb("a2", [F, 2], F32)
        g1 = sb("g1", [P, KT], F32)
        b1 = sb("b1", [P, KT], F32)
        g2 = sb("g2", [P, KT], F32)
        b2 = sb("b2", [P, KT], F32)
        fc1b = sb("fc1b", [P, HT], F32)
        small = small[:, 5 * NT:].rearrange("p (a n) -> p a n", n=NT)
        sd = small[:, 0:2, :]
        ac = small[:, 2:4, :]
        cols = small[:, 5:9, :]
        bd = small[:, 9:11, :]
        dmax = sb("dmax", [P, 3], F32)
        warm = sb("warm", [P, 2], F32)
        no_nb = sb("no_nb", [P, TB], F32)
        den1 = sb("den1", [P, TB], F32)
        rden = sb("rden", [P, TB], F32)

        sac_dram = nc.dram_tensor("sac_dram", (3, N), F32, kind="Internal").ap()

        banks = [bank(f"bank{i}") for i in range(8)]
        ps_t = banks[0:4]
        ps_wh = banks[4:6]
        ps_wa, ps_misc = banks[6:8]
        ps_dt, ps_dmax, _, ps_s = ps_t
        ps_pos, ps_neg, ps_den, ps_x = banks[0:4]
        ps_f = banks[4:6]
        ps_y = banks[6:8]

        consts_in = sem("consts_in")
        stage1_in = sem("stage1_in")
        stage2_in = sem("stage2_in")
        stage1_read = sem("stage1_read")
        stage2_read = sem("stage2_read")
        hi_copied = sem("hi_copied")
        full0_made = sem("full0_made")
        full_made = sem("full_made")
        row3_in = sem("row3_in")
        fcb_in = sem("fcb_in")
        carrier = sem("carrier")
        consts_set = sem("consts_set")
        prep_chain = sem("prep_chain")
        bias_mm = sem("bias_mm")
        xin_in = [sem(f"xin_in{i}") for i in range(RX)]
        xin_free = sem("xin_free")
        group_chain = sem("group_chain")
        var1 = sem("var1")
        rstd1 = sem("rstd1")
        xn1 = sem("xn1")
        xt1 = sem("xt1")
        h1 = sem("h1")
        wa_ps = sem("wa_ps")
        wa_sb = sem("wa_sb")
        wh_ps = sem("wh_ps")
        wh_sb = sem("wh_sb")
        dmax_part = sem("dmax_part")
        dmax_row = sem("dmax_row")
        dmax_one = sem("dmax_one")
        dmax_ps = sem("dmax_ps")
        dmax_all = sem("dmax_all")
        cols_set = sem("cols_set")
        exps_set = sem("exps_set")
        s_ps = sem("s_ps")
        ac_ps = sem("ac_ps")
        sact_sb = sem("sact_sb")
        sac_out = sem("sac_out")
        mean_ps = sem("mean_ps")
        split_chain = sem("split_chain")
        low_made = sem("low_made")
        weights_made = sem("weights_made")

        adj_in = [sem(f"adj_in{i}") for i in range(RA)]
        s_in = [sem("s_in0"), sem("s_in1")]
        s_free = sem("s_free")
        ac_in = sem("ac_in")
        ac_free = sem("ac_free")
        sign_made = sem("sign_made")
        signed = sem("signed")
        masks = sem("masks")
        masks_free = sem("masks_free")
        attn_ps = sem("attn_ps")
        attn_ps_free = sem("attn_ps_free")
        epi_chain = sem("epi_chain")
        den_parts = sem("den_parts")
        den_sum = sem("den_sum")
        den_read = sem("den_read")
        comb_made = sem("comb_made")
        comb_free = sem("comb_free")
        x_in = [sem("x_in0"), sem("x_in1")]
        xb_made = sem("xb_made")
        bias_chain = sem("bias_chain")
        bias3_made = sem("bias3_made")
        den_col = sem("den_col")
        den_col_read = sem("den_col_read")
        fc_ps = sem("fc_ps")
        x2_made = sem("x2_made")
        mlp_chain = sem("mlp_chain")
        var2 = sem("var2")
        rstd2 = sem("rstd2")
        xn2 = sem("xn2")
        xt2 = sem("xt2")
        h2hi_made = sem("h2hi_made")
        h2_made = sem("h2_made")
        f_ps = sem("f_ps")
        gelu_made = sem("gelu_made")
        m_made = sem("m_made")
        m_free = sem("m_free")
        y_ps = sem("y_ps")
        y_made = sem("y_made")
        out_done = [sem("out_done0"), sem("out_done1")]

        block = ctx.enter_context(nc.Block())

        CONSTS = 11

        def has_store(ib, half):
            return not isinstance(ib, int) or 0 <= 2 * ib - 4 + half < 2 * NB - 2

        def blocks(eng, emit):
            emit(0, 0, True, ((False, False), (False, False)))
            emit(1, 1, True, ((False, True), (True, True)))
            with eng.Fori(1, NB // 2) as bi:
                emit(bi * 2, 0, True, ((True, True), (True, True)))
                emit(bi * 2 + 1, 1, True, ((True, True), (True, True)))
            emit(NB, 0, False, ((True, True), (True, True)))
            emit(NB + 1, 1, False, ((True, False), (False, False)))

        @block.sync
        def _(sp):
            sp.dma_start(xin[0], x[0]).then_inc(xin_in[0], 16)
            for dst, src in ((ident[:, :], ident_in),
                             (wsb[:, :, 0:F], w.rearrange("(k p) n -> p k n", p=P)), (w_rows, w_t),
                             (a2[:, :], a),
                             (g1[:, :], ln1_g), (b1[:, :], ln1_b), (g2[:, :], ln2_g), (b2[:, :], ln2_b),
                             (fc1b[:, :], fc1_b),
                             (fcw2[0:F, :], fc_wt), (fcw2[F:P, :], fc_wt)):
                sp.dma_start(dst, src).then_inc(consts_in, 16)

            for g in range(1, RX):
                sp.dma_start(xin[g], x[g]).then_inc(xin_in[g], 16)
            with sp.Fori(1, NB // RX) as gi:
                for par in range(RX):
                    g = gi * RX + par
                    sp.wait_ge(xin_free, g + (1 - RX))
                    sp.dma_start(xin[par], x[bass.ds(g, 1)].rearrange("g p t n -> (g p) t n")
                                 ).then_inc(xin_in[par], 16)

            def load_adj(ib, q):
                sp.wait_ge(signed, ib * NQ + (q + 1))
                sp.dma_start(adj_ring[:, q % RA, :],
                             adj_tiles[bass.ds(ib, 1), q].rearrange("b p n -> (b p) n")
                             ).then_inc(adj_in[q % RA], 16)

            for q in range(RA):
                load_adj(0, q)
            sp.wait_ge(sact_sb, 1)
            sp.dma_start(sac_dram[0].rearrange("(t p) -> t p", p=P), sact[:, 0, :]).then_inc(sac_out, 16)
            sp.wait_ge(sac_out, 16)
            sp.dma_start(s_bc[:, 0, :], sac_dram[0:1, 0:BLK].broadcast_to([P, BLK])).then_inc(s_in[0], 16)
            sp.wait_ge(sact_sb, 3)
            for c in range(1, 3):
                sp.dma_start(sac_dram[c].rearrange("(t p) -> t p", p=P), sact[:, c, :]).then_inc(sac_out, 16)

            def block_sp(ib, par, attn, steps):
                first = isinstance(ib, int) and ib == 0
                for q in range(NQ):
                    half, c = divmod(q, HALF)
                    back, front = steps[half]
                    n = 2 * ib - 3 + half
                    if attn and not (first and q < RA):
                        load_adj(ib, q)
                    if first and q == STAGE1_AT:
                        sp.wait_ge(weights_made, NT // WT)
                        sp.wait_ge(mean_ps, 1)
                        sp.dma_start(stage1, fc1_wt.rearrange("(k p) n -> p k n", p=P)).then_inc(stage1_in, 16)
                    if first and q == STAGE2_AT:
                        sp.wait_ge(stage1_read, 1)
                        sp.wait_ge(bias_mm, 1)
                        sp.dma_start(stage2, fc2_wt.rearrange("(k p) n -> p k n", p=P)).then_inc(stage2_in, 16)
                    if first and q == ROW3_AT:
                        sp.wait_ge(sac_out, 48)
                        sp.dma_start(row3, fc2_b.broadcast_to([3, D])).then_inc(row3_in, 16)
                    if first and q == FCB_AT:
                        sp.wait_ge(stage2_read, 2)
                        sp.dma_start(fcb_bc, fc_b.broadcast_to([P, D])).then_inc(fcb_in, 16)
                    if attn and q == 3 * NQ // 4:
                        if first:
                            sp.wait_ge(bias3_made, 1)
                        sp.wait_ge(ac_free, ib + 1)
                        for k, dst in ((1, a_bc), (2, c_bc)):
                            sp.dma_start(dst, sac_dram[k:k + 1, bass.ds(ib * BLK, BLK)]
                                         .broadcast_to([P, BLK])).then_inc(ac_in, 16)
                        sp.wait_ge(s_free, ib + 1)
                        nxt = (ib + 1) % NB
                        sp.dma_start(s_bc[:, 1 - par, :], sac_dram[0:1, bass.ds(nxt * BLK, BLK)]
                                     .broadcast_to([P, BLK])).then_inc(s_in[1 - par], 16)
                    odd = half % 2
                    if c == STORE_AT and has_store(ib, half):
                        sp.wait_ge(y_made, n * TS + TS)
                        sp.sem_inc(carrier, 1)
                        sp.dma_start(out[bass.ds(ib - 2, 1), :, half * TS:(half + 1) * TS]
                                     .rearrange("g p t d -> (g p) t d"), x2[odd]
                                     ).then_inc(out_done[odd], 16)
                    if c == LOAD_AT and front:
                        if has_store(ib, half):
                            sp.wait_ge(out_done[odd], (ib - 1) * 16)
                            sp.sem_inc(carrier, 1)
                        sp.dma_start(x2[odd], x[bass.ds(ib - 1, 1), :, half * TS:(half + 1) * TS]
                                     .rearrange("g p t d -> (g p) t d")
                                     ).then_inc(x_in[odd], 16)

            blocks(sp, block_sp)
            for n in range(2 * NB - 2, 2 * NB):
                sp.wait_ge(y_made, n * TS + 2 * TS)
                sp.dma_start(out[NB - 1, :, n % NS * TS:(n % NS + 1) * TS], x2[n % 2]).then_inc(out_done[n % 2], 16)
            for odd in range(2):
                sp.wait_ge(out_done[odd], NB * 16)
            sp.wait_ge(s_in[0], (NB // 2 + 1) * 16)

        @block.gpsimd
        def _(pool):
            pool.memset(warm[:, :], 0.0).then_inc(consts_set, 1)
            pool.memset(ones[:, :], 1.0).then_inc(consts_set, 1)
            pool.memset(minus_half[:, :], -0.5).then_inc(consts_set, 1)
            pool.wait_ge(consts_set, 4)
            with pool.Fori(0, NB // 2) as gi:
                for par in range(2):
                    pool.wait_ge(var1, gi * 2 + (par + 1))
                    pool.tensor_tensor(rstd_2[:, par, :], var_eps[:, :], minus_half[:, :], ALU.pow
                                       ).then_inc(rstd1, 1)
            pool.wait_ge(wh_sb, 2 * NB + 4)
            pool.wait_ge(exps_set, 2)
            for p in range(1, NT // WT):
                for c in range(2):
                    tiles = slice(p * WT, (p + 1) * WT)
                    pool.tensor_tensor(full[c][:, tiles, :], wh_all[:, tiles, :],
                                       bd[:, c, tiles].unsqueeze(2).broadcast_to([P, WT, F]), ALU.mult
                                       ).then_inc(full_made, 1)

            pool.wait_ge(prep_chain, KT + 1)
            pool.tensor_tensor(fc2_lo[:, 0:HT // 2, :], stage2[:, 0:HT // 2, :],
                               fc2_hi[:, 0:HT // 2, :].bitcast(F32), ALU.subtract).then_inc(stage2_read, 1)

            def block_pool(ib, par, attn, steps):
                for half in range(NS):
                    back, front = steps[half]
                    n = 2 * ib - 3 + half
                    odd = half % 2
                    for c in range(HALF):
                        if front and c == BIAS_AT:
                            if isinstance(ib, int) and ib == 1:
                                pool.wait_ge(fcb_in, 16)
                            pool.wait_ge(x_in[odd], ib * 16)
                            for t in range(TS):
                                pool.tensor_tensor(x2[odd][:, t, :], x2[odd][:, t, :], fcb_bc, ALU.add
                                                   ).then_inc(xb_made, 1)
                        for t in range(TS):
                            if front and c == X2_AT[t]:
                                pool.wait_ge(var2, n * TS + (TS + t + 1))
                                pool.tensor_tensor(rstd[:, t:t + 1], var_eps[:, t:t + 1],
                                                   minus_half[:, t:t + 1], ALU.pow).then_inc(rstd2, 1)
                        for h in range(HT):
                            if back and c == SPLIT_AT[h]:
                                pool.wait_ge(gelu_made, n * HT + (h + 3))
                                pool.tensor_tensor(m_lo[:, h % 2, :], gl[:, h % 2, :],
                                                   m_hi[:, h % 2, :].bitcast(F32), ALU.subtract
                                                   ).then_inc(m_made, 1)

            blocks(pool, block_pool)

        @block.scalar
        def _(act):
            act.sem_inc(masks, 2 * RM)
            act.sem_inc(wh_sb, 4)
            act.sem_inc(gelu_made, 2)
            act.wait_ge(consts_in, 16 * CONSTS)
            act.wait_ge(consts_set, 4)

            act.wait_ge(wa_ps, 1)
            act.copy(wsb[:, :, F:FE], ps_wa[:, 0:2 * KT].rearrange("p (k c) -> p k c", c=2)).then_inc(wa_sb, 1)

            def keep(g, par):
                act.wait_ge(wh_ps, g + 1)
                src = ps_wh[par][:, 0:TB * FE].rearrange("p (t c) -> p t c", c=FE)
                act.copy(wh_all[:, bass.ds(g * TB, TB), :], src[:, :, 0:F]).then_inc(wh_sb, 1)
                act.copy(sd[:, :, bass.ds(g * TB, TB)], src[:, :, F:FE].rearrange("p t c -> p c t")
                         ).then_inc(wh_sb, 1)

            def project_act(g, par):
                for k in range(KT):
                    act.wait_ge(xt1, g * KT + (k + 1))
                    act.activation(ht[:, k, :], ps_t[k][:, :], ACT.Identity, bias=b1[:, k:k + 1],
                                   scale=g1[:, k:k + 1]).then_inc(h1, 1)
                    if k == 1 and not (isinstance(g, int) and g == 0):
                        keep(g - 1, 1 - par)

            for g in range(2):
                project_act(g, g)
            with act.Fori(1, NB // 2) as gi:
                for par in range(2):
                    project_act(gi * 2 + par, par)
            keep(NB - 1, 1)
            act.activation(warm[:, 1:2], warm[:, 0:1], ACT.Exp)
            act.wait_ge(s_ps, 1)
            act.copy(sact[:, 0, :], ps_s[0:NT, 0:P]).then_inc(sact_sb, 1)
            act.wait_ge(cols_set, 3)
            act.activation(bd[:, 0, :], cols[:, 0, :], ACT.Exp).then_inc(exps_set, 1)
            act.activation(bd[:, 1, :], cols[:, 0, :], ACT.Exp, scale=SLOPE).then_inc(exps_set, 1)
            act.activation(ac[:, 0, :], cols[:, 1, :], ACT.Exp, scale=1 - SLOPE).then_inc(exps_set, 1)
            act.activation(ac[:, 1, :], cols[:, 2, :], ACT.Exp, scale=SLOPE - 1).then_inc(exps_set, 1)
            act.wait_ge(ac_ps, 1)
            for c in range(2):
                act.copy(sact[:, 1 + c, :], ps_misc[0:NT, c * P:(c + 1) * P]).then_inc(sact_sb, 1)

            def high_weights(p):
                tiles = slice(p * WT, (p + 1) * WT)
                for c, wdst in enumerate((wpos, wneg)):
                    if p == 0:
                        act.wait_ge(full0_made, c + 1)
                    else:
                        act.wait_ge(full_made, 2 * (p - 1) + c + 1)
                    act.copy(wdst[:, tiles, 0:F], full[c][:, tiles, :]).then_inc(hi_copied, 1)

            def block_act(ib, par, attn, steps):
                act.activation(warm[:, 1:2], warm[:, 0:1], ACT.Gelu)
                for q in range(NQ):
                    half, c = divmod(q, HALF)
                    back, front = steps[half]
                    n = 2 * ib - 3 + half
                    if isinstance(ib, int) and ib == 0 and q in WEIGHTS_AT:
                        high_weights(WEIGHTS_AT.index(q))
                    if attn:
                        act.wait_ge(signed, ib * NQ + (q + (RA + 1)))
                        act.wait_ge(masks_free, ib * NQ + (q + 1))
                        src = sign_ring[:, q % RM, :]
                        act.activation(mpos[:, q % RM, :], src, ACT.Relu, scale=2.0).then_inc(masks, 1)
                        act.activation(mneg[:, q % RM, :], src, ACT.Relu, scale=-2.0).then_inc(masks, 1)
                    for h in range(HT):
                        if back and c == GELU_AT[h]:
                            act.wait_ge(f_ps, n * HT + (h + 2))
                            act.wait_ge(m_made, n * HT + (h + 1))
                            act.wait_ge(m_free, n * HT + (h + 1))
                            act.activation(gl[:, h % 2, :], ps_f[h % 2][:, 0:SUB], ACT.Gelu,
                                           bias=fc1_bias[:, h:h + 1])
                            act.activation(m_hi[:, h % 2, :], ps_f[h % 2][:, 0:SUB], ACT.Gelu,
                                           bias=fc1_bias[:, h:h + 1]).then_inc(gelu_made, 1)
                    for t in range(TS):
                        if front and c == HI_AT[t]:
                            act.wait_ge(xt2, n * TS + (TS + t + 2))
                            if t == 0:
                                act.wait_ge(f_ps, n * HT + (HT + 1))
                            act.copy(h2_hi[:, :, t * P:(t + 1) * P],
                                     ps_x[:, :].rearrange("p (k n) -> p k n", k=KT)).then_inc(h2hi_made, 1)

            blocks(act, block_act)

        @block.vector
        def _(dve):
            dve.memset(mean_wh[:, :], 0.0).then_inc(consts_set, 1)
            dve.sem_inc(signed, RA)
            dve.sem_inc(ac_free, 1)
            dve.sem_inc(s_free, 1)
            dve.sem_inc(m_made, 2)
            dve.sem_inc(rstd1, 1)
            dve.sem_inc(attn_ps_free, 1)
            dve.sem_inc(y_made, TS)
            dve.sem_inc(h2_made, 1)

            def group_stats(g, turn, par):
                dve.wait_ge(xin_in[par], turn * 16 + 16)
                for t in range(TB):
                    ins = dve.bn_stats(stats_2[:, par % 2, t, :], xin[par][:, t, :])
                ins.then_inc(group_chain, 1)

            def group_variance(g, par):
                base = g * GROUP_CHAIN
                dve.wait_ge(group_chain, base + 1)
                dve.sem_inc(carrier, 1)
                for t in range(TB):
                    ins = dve.bn_aggr(mv_2[:, par % 2, t, :], stats_2[:, par % 2, t, :])
                ins.then_inc(group_chain, 1)
                dve.wait_ge(group_chain, base + 2)
                dve.wait_ge(rstd1, g + 1)
                dve.tensor_scalar(var_eps[:, :], mv_2[:, par % 2, :, 1], EPS, None, ALU.add).then_inc(var1, 1)

            def group_rows(g, par):
                dve.wait_ge(rstd1, g + 2)
                for t in range(TB):
                    ins = dve.tensor_scalar(xin[par][:, t, :], xin[par][:, t, :], mv_2[:, par % 2, t, 0:1],
                                            rstd_2[:, par % 2, t:t + 1], ALU.subtract, ALU.mult)
                ins.then_inc(xn1, 1)

            group_stats(0, 0, 0)
            group_variance(0, 0)
            with dve.Fori(0, NB // RX - 1) as gi:
                for par in range(RX):
                    g = gi * RX + par
                    group_stats(g + 1, gi + (par + 1) // RX, (par + 1) % RX)
                    group_rows(g, par)
                    group_variance(g + 1, (par + 1) % RX)
            for g in range(NB - RX, NB):
                if g + 1 < NB:
                    group_stats(g + 1, (g + 1) // RX, (g + 1) % RX)
                group_rows(g, g % RX)
                if g + 1 < NB:
                    group_variance(g + 1, (g + 1) % RX)

            dve.wait_ge(wh_sb, 2 * NB + 4)
            dve.tensor_reduce(dmax[:, 0:1], sd[:, 1, :], AX_X, ALU.max).then_inc(dmax_part, 1)
            dve.tensor_scalar(negd[:, :], sd[:, 1, :], -1.0, None, ALU.mult).then_inc(split_chain, 1)
            dve.memset(ps_den[:, :], 0.0).then_inc(split_chain, 1)
            dve.wait_ge(dmax_row, 1)
            dve.tensor_reduce(dmax[0:1, 1:2], ps_dt[0:1, 0:P], AX_X, ALU.max).then_inc(dmax_one, 1)
            dve.wait_ge(dmax_ps, 1)
            dve.tensor_copy(dmax[:, 2:3], ps_dmax[:, 0:1]).then_inc(dmax_all, 1)
            dve.wait_ge(dmax_all, 1)
            dve.tensor_scalar(cols[:, 0, :], sd[:, 1, :], dmax[:, 2:3], None, ALU.subtract).then_inc(cols_set, 1)
            dve.tensor_scalar(cols[:, 1, :], sd[:, 0, :], dmax[:, 2:3], 0.0, ALU.add, ALU.min).then_inc(cols_set, 1)
            dve.tensor_scalar(cols[:, 2, :], sd[:, 0, :], dmax[:, 2:3], 0.0, ALU.add, ALU.max).then_inc(cols_set, 1)
            dve.wait_ge(exps_set, 2)
            for c in range(2):
                dve.tensor_tensor(full[c][:, 0:WT, :], wh_all[:, 0:WT, :],
                                  bd[:, c, 0:WT].unsqueeze(2).broadcast_to([P, WT, F]), ALU.mult
                                  ).then_inc(full0_made, 1)
            dve.wait_ge(exps_set, 4)
            step = 2
            for i in range(3):
                for c, ddst in enumerate((den_pos, den_neg)):
                    src = bd[:, c, :] if i == 0 else cols[:, c, :]
                    dve.tensor_copy(ddst[:, :, i], src).then_inc(split_chain, 1)
                step += 2
                dve.wait_ge(split_chain, step)
                if i < 2:
                    for c, ddst in enumerate((den_pos, den_neg)):
                        src = bd[:, c, :] if i == 0 else cols[:, c, :]
                        dve.tensor_tensor(cols[:, c, :], src, ddst[:, :, i], ALU.subtract).then_inc(split_chain, 1)
                    step += 2
                    dve.wait_ge(split_chain, step)

            def low_weights(p):
                tiles = slice(p * WT, (p + 1) * WT)
                for c, wdst in enumerate((wpos, wneg)):
                    dve.wait_ge(hi_copied, 2 * p + c + 1)
                    dve.tensor_tensor(wdst[:, tiles, F:2 * F], full[c][:, tiles, :],
                                      wdst[:, tiles, 0:F].bitcast(F32), ALU.subtract).then_inc(low_made, 1)
                dve.wait_ge(low_made, 2 * p + 2)
                dve.sem_inc(weights_made, 1)
                if p == NT // WT - 1:
                    dve.wait_ge(mean_ps, 1)
                    dve.tensor_scalar(mean_wh[0:F, :], ps_wh[0][0:F, 0:1], 1.0 / N, None, ALU.mult
                                      ).then_inc(split_chain, 1)
                    dve.wait_ge(split_chain, step + 1)

            def prepare(q):
                if q == FC1_PREP_AT:
                    dve.wait_ge(stage1_in, 16)
                    for k in range(KT):
                        dve.tensor_scalar(fc1_hi[:, k, :], stage1[:, k, :], g2[:, k:k + 1], None, ALU.mult
                                          ).then_inc(prep_chain, 1)
                if q == FC1_PREP_AT + 2:
                    dve.wait_ge(prep_chain, KT)
                    for k in range(KT):
                        ins = dve.scalar_tensor_tensor(out=fc1_lo[:, k, :], in0=stage1[:, k, :],
                                                       scalar=g2[:, k:k + 1], in1=fc1_hi[:, k, :].bitcast(F32),
                                                       op0=ALU.mult, op1=ALU.subtract)
                    ins.then_inc(stage1_read, 1)
                if q == FC2_PREP_AT:
                    dve.wait_ge(bias_mm, 1)
                    dve.tensor_tensor(fc1_bias[:, :], ps_y[0][:, 0:HT], fc1b[:, :], ALU.add).then_inc(bias_chain, 1)
                    dve.wait_ge(stage2_in, 16)
                    for i in range(2):
                        part_h = slice(i * HT // 2, (i + 1) * HT // 2)
                        dve.tensor_copy(fc2_hi[:, part_h, :], stage2[:, part_h, :]).then_inc(prep_chain, 1)
                if q == FC2_PREP_AT + 2:
                    dve.wait_ge(prep_chain, KT + 2)
                    dve.tensor_tensor(fc2_lo[:, HT // 2:, :], stage2[:, HT // 2:, :],
                                      fc2_hi[:, HT // 2:, :].bitcast(F32), ALU.subtract).then_inc(stage2_read, 1)
                if q == BIAS3_AT:
                    dve.wait_ge(row3_in, 16)
                    dve.memset(ones3, 1.0).then_inc(bias_chain, 1)
                    for p3 in range(3):
                        dve.tensor_copy(tail3, row3).then_inc(bias_chain, 1)
                        dve.wait_ge(bias_chain, 1 + 3 * p3 + 1)
                        if p3 == 0:
                            dve.tensor_scalar(bias3[0:3, :], tail3, ident[0:3, 0:1], None, ALU.mult
                                              ).then_inc(bias_chain, 1)
                        else:
                            dve.scalar_tensor_tensor(out=bias3[0:3, :], in0=tail3, scalar=ident[0:3, p3:p3 + 1],
                                                     in1=bias3[0:3, :], op0=ALU.mult, op1=ALU.add
                                                     ).then_inc(bias_chain, 1)
                        dve.tensor_tensor(row3, row3, tail3, ALU.subtract).then_inc(bias_chain, 1)
                        dve.wait_ge(bias_chain, 1 + 3 * p3 + 3)
                    dve.sem_inc(bias3_made, 1)

            def s_loads(ib, par):
                if isinstance(ib, int):
                    return (ib // 2 + 1) * 16
                return (ib - par) * 8 + 16

            def sign(ib, par, q):
                dve.wait_ge(masks, ib * (2 * NQ) + (2 * q + 2))
                for u in range(PAIR):
                    j = PAIR * q + u
                    ins = dve.tensor_scalar(sign_ring[:, q % RM, u * BLK:(u + 1) * BLK], s_bc[:, par, :],
                                            negd[:, j:j + 1], 0.5, ALU.is_ge, ALU.subtract)
                ins.then_inc(sign_made, 1)
                if q == NQ - 1:
                    dve.wait_ge(sign_made, ib * NQ + NQ)
                    dve.sem_inc(s_free, 1)

            def mask_sign(ib, q):
                k = ib * NQ + q
                dve.wait_ge(sign_made, k + 1)
                dve.wait_ge(adj_in[q % RA], ib * (16 * NQ // RA) + 16 * (q // RA + 1))
                dve.scalar_tensor_tensor(out=sign_ring[:, q % RM, :], in0=adj_ring[:, q % RA, :], scalar=0.0,
                                         in1=sign_ring[:, q % RM, :], op0=ALU.is_gt, op1=ALU.mult
                                         ).then_inc(signed, 1)

            def epilogue(ib, q):
                e = ib * EPI_CHAIN
                if q == 0:
                    dve.wait_ge(attn_ps, ib + 1)
                    dve.wait_ge(ac_in, ib * 32 + 32)
                    dve.wait_ge(comb_free, ib + 1)
                    dve.tensor_tensor(comb, a_bc, ps_pos[:, :], ALU.mult).then_inc(epi_chain, 1)
                    dve.tensor_tensor(tmp, c_bc, ps_neg[:, :], ALU.mult).then_inc(epi_chain, 1)
                    dve.wait_ge(epi_chain, e + 1)
                    h = P // 2
                    dve.tensor_tensor(a_bc[0:h, :], a_bc[0:h, :], ps_den[0:h, :], ALU.mult).then_inc(den_parts, 1)
                    dve.tensor_tensor(a_bc[h:P, :], c_bc[h:P, :], ps_den[h:P, :], ALU.mult).then_inc(den_parts, 1)
                if q == 1:
                    dve.wait_ge(den_parts, ib * 2 + 2)
                    dve.sem_inc(attn_ps_free, 1)
                    dve.wait_ge(epi_chain, e + 2)
                    dve.tensor_tensor(comb, comb, tmp, ALU.add).then_inc(epi_chain, 1)
                if q == 3:
                    dve.wait_ge(den_col, ib + 1)
                    dve.tensor_scalar(no_nb[:, :], ps_x[:, 0:TB], 0.0, None, ALU.is_equal).then_inc(epi_chain, 1)
                    dve.wait_ge(epi_chain, e + 4)
                    dve.tensor_tensor(den1[:, :], no_nb[:, :], ps_x[:, 0:TB], ALU.add).then_inc(epi_chain, 1)
                    dve.wait_ge(epi_chain, e + 5)
                    dve.sem_inc(den_col_read, 1)
                    dve.reciprocal(rden[:, :], den1[:, :]).then_inc(epi_chain, 1)
                if q == 5:
                    dve.wait_ge(den_sum, ib + 1)
                    dve.tensor_scalar(c_bc, ps_x[:, :], 0.0, None, ALU.is_equal).then_inc(den_read, 1)
                    dve.wait_ge(den_read, ib + 1)
                    dve.wait_ge(epi_chain, e + 6)
                    dve.scalar_tensor_tensor(out=comb, in0=c_bc, scalar=mean_wh[:, 0:1], in1=comb,
                                             op0=ALU.mult, op1=ALU.add).then_inc(comb_made, 1)
                    dve.wait_ge(comb_made, ib + 1)
                    dve.sem_inc(ac_free, 1)

            def rows_and_stats(n, half, t):
                slot, tile = x2[half][:, t, :], TS * half + t
                c = n * (TS * MLP_CHAIN) + t * MLP_CHAIN
                dve.wait_ge(xb_made, n * TS + (t + 1))
                dve.wait_ge(fc_ps, n * TS + (t + 1))
                dve.scalar_tensor_tensor(out=slot, in0=ps_x[:, :], scalar=rden[:, tile:tile + 1], in1=slot,
                                         op0=ALU.mult, op1=ALU.add).then_inc(x2_made, 1)
                dve.wait_ge(x2_made, n * TS + (t + 1))
                dve.bn_stats(stats[:, t, :], slot).then_inc(mlp_chain, 1)
                dve.wait_ge(mlp_chain, c + 1)
                dve.sem_inc(carrier, 1)
                dve.bn_aggr(mv[:, t, :], stats[:, t, :]).then_inc(mlp_chain, 1)
                dve.wait_ge(mlp_chain, c + 2)
                dve.tensor_scalar(var_eps[:, t:t + 1], mv[:, t, 1:2], EPS, None, ALU.add).then_inc(var2, 1)

            def normalise(n, half, t):
                dve.wait_ge(rstd2, n * TS + (t + 1))
                dve.wait_ge(xt2, n * TS + (t + 1))
                dve.tensor_scalar(xn, x2[half][:, t, :], mv[:, t, 0:1], rstd[:, t:t + 1],
                                  ALU.subtract, ALU.mult).then_inc(xn2, 1)

            def low_half(n, t):
                dve.wait_ge(h2hi_made, n * TS + (t + 1))
                cut = slice(t * P, (t + 1) * P)
                dve.tensor_tensor(h2_lo[:, :, cut], ps_x[:, :].rearrange("p (k n) -> p k n", k=KT),
                                  h2_hi[:, :, cut].bitcast(F32), ALU.subtract).then_inc(h2_made, 1)

            def finish_rows(n, half):
                dve.wait_ge(y_ps, n + 1)
                for t in range(TS):
                    slot = x2[1 - half][:, t, :]
                    dve.tensor_tensor(slot, ps_y[t][:, :], slot, ALU.add).then_inc(y_made, 1)

            def block_dve(ib, par, attn, steps):
                if attn:
                    dve.wait_ge(s_in[par], s_loads(ib, par))
                    sign(ib, par, 0)
                for q in range(NQ):
                    half, c = divmod(q, HALF)
                    back, front = steps[half]
                    n = 2 * ib - 3 + half
                    if attn:
                        mask_sign(ib, q)
                        if q + 1 < NQ:
                            sign(ib, par, q + 1)
                    if isinstance(ib, int) and ib == 0:
                        if q in WEIGHTS_AT:
                            low_weights(WEIGHTS_AT.index(q))
                        prepare(q)
                    if steps[0][1]:
                        epilogue(ib - 1, q)
                    for t in range(TS):
                        if front and c == LO_AT[t]:
                            low_half(n + 1, t)
                        if front and c == X2_AT[t]:
                            rows_and_stats(n + 1, half, t)
                        if front and c == XN_AT[t]:
                            normalise(n + 1, half, t)
                    if back and c == Y_AT:
                        finish_rows(n, half)

            blocks(dve, block_dve)

        @block.tensor
        def _(pe):
            pe.sem_inc(masks_free, RM)
            pe.sem_inc(f_ps, 1)
            pe.sem_inc(m_free, 2)
            pe.sem_inc(comb_free, 1)
            pe.sem_inc(xt2, 1)
            pe.wait_ge(consts_in, 16 * CONSTS)

            def transpose_group(g, par, k):
                if k == 0:
                    pe.wait_ge(xn1, g + 1)
                for t in range(TB):
                    ins = pe.transpose(ps_t[k][:, t * P:(t + 1) * P], xin[par][:, t, k * P:(k + 1) * P],
                                       ident[:, :])
                ins.then_inc(xt1, 1)
                if k == KT - 1:
                    pe.wait_ge(xt1, g * KT + KT)
                    pe.sem_inc(xin_free, 1)

            def project(g, par):
                pe.wait_ge(wh_sb, g * 2 + 2)
                for k in range(KT):
                    pe.wait_ge(h1, g * KT + (k + 1))
                    for t in range(TB):
                        ins = pe.matmul(ps_wh[par % 2][:, t * FE:(t + 1) * FE], ht[:, k, t * P:(t + 1) * P],
                                        wsb[:, k, :], start=(k == 0 and t == 0),
                                        stop=(k == KT - 1 and t == TB - 1))
                    if k == KT - 1:
                        ins.then_inc(wh_ps, 1)
                    if not (isinstance(g, int) and g == NB - 1):
                        transpose_group(g + 1, (par + 1) % RX, k)

            for k in range(KT):
                ins = pe.matmul(ps_wa[:, 2 * k:2 * k + 2], w_rows[:, k * P:(k + 1) * P], a2[:, :],
                                start=True, stop=True)
            ins.then_inc(wa_ps, 1)
            for k in range(KT):
                transpose_group(0, 0, k)
            pe.wait_ge(wa_sb, 1)
            with pe.Fori(0, NB // RX - 1) as gi:
                for par in range(RX):
                    project(gi * RX + par, par)
            for g in range(NB - RX, NB):
                project(g, g % RX)

            pe.wait_ge(wh_sb, 2 * NB + 4)
            pe.transpose(ps_s[0:NT, 0:P], sd[:, 0, :], ident[:, :]).then_inc(s_ps, 1)
            pe.wait_ge(dmax_part, 1)
            pe.transpose(ps_dt[0:1, 0:P], dmax[:, 0:1], ident[:, :]).then_inc(dmax_row, 1)
            pe.wait_ge(consts_set, 4)
            pe.wait_ge(dmax_one, 1)
            pe.matmul(ps_dmax[:, 0:1], ones[0:1, :], dmax[0:1, 1:2], start=True, stop=True).then_inc(dmax_ps, 1)
            for t in range(NT):
                ins = pe.matmul(ps_wh[0][0:F, 0:1], wh_all[:, t, :], ones[:, 0:1], start=(t == 0), stop=(t == NT - 1))
            ins.then_inc(mean_ps, 1)
            pe.wait_ge(exps_set, 4)
            for c in range(2):
                ins = pe.transpose(ps_misc[0:NT, c * P:(c + 1) * P], ac[:, c, :], ident[:, :])
            ins.then_inc(ac_ps, 1)

            def attention(ib, q):
                pe.wait_ge(masks, ib * (2 * NQ) + (2 * q + 6))
                if isinstance(ib, int) and ib == 0 and q % (WT // PAIR) == 0:
                    pe.wait_ge(weights_made, q // (WT // PAIR) + 1)
                if q == 0:
                    pe.wait_ge(attn_ps_free, ib + 1)
                r = q % RM
                for u in range(PAIR):
                    j = PAIR * q + u
                    cut = slice(u * BLK, (u + 1) * BLK)
                    pe.matmul(ps_pos[:, :], wpos[:, j, :], mpos[:, r, cut], start=(j == 0), stop=(j == NT - 1))
                    pe.matmul(ps_neg[:, :], wneg[:, j, :], mneg[:, r, cut], start=(j == 0), stop=(j == NT - 1))
                for c, (m, dw) in enumerate(((mpos, den_pos), (mneg, den_neg))):
                    for u in range(PAIR):
                        j = PAIR * q + u
                        o = 32 * (2 * c + u)
                        half = m[:, r, u * BLK:(u + 1) * BLK].bitcast(BF16)[:, 1::2]
                        ins = pe.matmul(ps_den[o:o + 3, :], dw[:, j, :], half, start=(q == 0), stop=(q == NQ - 1),
                                        tile_position=(0, o))
                ins.then_inc(masks_free, 1)
                if q == NQ - 1:
                    pe.wait_ge(masks_free, ib * NQ + (NQ + RM))
                    pe.sem_inc(attn_ps, 1)

            def denominators(ib, q):
                if q == 1:
                    pe.wait_ge(den_parts, ib * 2 + 2)
                    for t in range(TB):
                        ins = pe.matmul(ps_x[:, t:t + 1], a_bc[:, t * P:(t + 1) * P], ones[:, 0:1],
                                        start=True, stop=True)
                    ins.then_inc(den_col, 1)
                if q == 3:
                    pe.wait_ge(den_col_read, ib + 1)
                    pe.matmul(ps_x[:, :], ones[:, :], a_bc, start=True, stop=True).then_inc(den_sum, 1)

            def fc(ib, n, half, t):
                pe.wait_ge(comb_made, ib + 1)
                if t > 0:
                    pe.wait_ge(x2_made, n * TS + t)
                c = (half * TS + t) * P
                pe.matmul(ps_x[:, :], comb[:, c:c + P], fcw2[:, :], start=True, stop=True).then_inc(fc_ps, 1)
                if half == NS - 1 and t == TS - 1:
                    pe.wait_ge(fc_ps, n * TS + TS)
                    pe.sem_inc(comb_free, 1)

            def transpose_rows(n, t):
                pe.wait_ge(xn2, n * TS + (t + 1))
                if t == 0:
                    pe.wait_ge(x2_made, n * TS + TS)
                pe.wait_ge(h2_made, n * TS + (t + 1))
                for k in range(KT):
                    ins = pe.transpose(ps_x[:, k * P:(k + 1) * P], xn[:, k * P:(k + 1) * P], ident[:, :])
                ins.then_inc(xt2, 1)

            def fc1(n, h):
                if h == 0:
                    pe.wait_ge(h2_made, n * TS + (TS + 1))
                pe.wait_ge(gelu_made, n * HT + (h + 1))
                cut = slice(h * P, (h + 1) * P)
                i = 0
                for wt, v in ((fc1_hi, h2_hi), (fc1_lo, h2_hi), (fc1_hi, h2_lo)):
                    for k in range(KT):
                        ins = pe.matmul(ps_f[h % 2][:, 0:SUB], wt[:, k, cut], v[:, k, :],
                                        start=(i == 0), stop=(i == 3 * KT - 1))
                        i += 1
                ins.then_inc(f_ps, 1)

            def fc2(ib, n, h):
                if h == 0:
                    pe.wait_ge(y_made, n * TS + TS)
                    if isinstance(ib, int) and ib == 1:
                        pe.wait_ge(bias3_made, 1)
                    for t in range(TS):
                        pe.matmul(ps_y[t][:, :], ones3[0:3, :], bias3[0:3, :], start=True, stop=False)
                pe.wait_ge(m_made, n * HT + (h + 3))
                for t in range(TS):
                    cut = slice(t * P, (t + 1) * P)
                    for i, (m, wt) in enumerate(((m_hi, fc2_hi), (m_hi, fc2_lo), (m_lo, fc2_hi))):
                        ins = pe.matmul(ps_y[t][:, :], m[:, h % 2, cut], wt[:, h, :],
                                        start=False, stop=(h == HT - 1 and i == 2))
                ins.then_inc(m_free, 1)
                if h == HT - 1:
                    pe.wait_ge(m_free, n * HT + (HT + 2))
                    pe.sem_inc(y_ps, 1)

            def block_pe(ib, par, attn, steps):
                for q in range(NQ):
                    half, c = divmod(q, HALF)
                    back, front = steps[half]
                    n = 2 * ib - 3 + half
                    for h in range(HT):
                        if back and c == FC2_AT[h]:
                            fc2(ib, n, h)
                        if back and c == FC1_AT[h]:
                            fc1(n, h)
                    if isinstance(ib, int) and ib == 0 and BIAS_MM_AT <= q < BIAS_MM_AT + HT:
                        h = q - BIAS_MM_AT
                        pe.wait_ge(stage1_in, 16)
                        for k in range(KT):
                            ins = pe.matmul(ps_y[0][:, h:h + 1], stage1[:, k, h * P:(h + 1) * P],
                                            b2[:, k:k + 1], start=(k == 0), stop=(k == KT - 1))
                        if h == HT - 1:
                            ins.then_inc(bias_mm, 1)
                    if steps[0][1]:
                        denominators(ib - 1, q)
                    for t in range(TS):
                        if front and c == XT_AT[t]:
                            transpose_rows(n + 1, t)
                        if front and c == FC_AT[t]:
                            fc(ib - 1, n + 1, half, t)
                    if attn:
                        attention(ib, q)

            blocks(pe, block_pe)


def kernel(**inputs):
    import concourse.bacc as bacc
    from concourse.bass_utils import run_bass_kernel_spmd

    nc = bacc.Bacc("TRN2", target_bir_lowering=False, num_devices=1)
    g = {k.replace("L0_gnn_", ""): np.asarray(v) for k, v in inputs.items()}
    adj = g["adj"].reshape(NB, BLK, NQ, PAIR, P).transpose(0, 2, 4, 3, 1).reshape(NB, NQ, P, PAIR * BLK)

    x = g["x"].reshape(NB, TB, P, D).transpose(0, 2, 1, 3)

    def columns(v):
        return v.reshape(-1, P).T

    arrays = {
        "x": x, "adj_tiles": adj, "w": g["W"], "w_t": g["W"].T, "a": g["a"].reshape(2, F).T,
        "fc_wt": g["fc_w"].T, "fc_b": g["fc_b"].reshape(1, D),
        "ln1_g": columns(g["ln1_g"]), "ln1_b": columns(g["ln1_b"]),
        "ln2_g": columns(g["ln2_g"]), "ln2_b": columns(g["ln2_b"]),
        "fc1_wt": g["fc1_w"].T, "fc1_b": columns(g["fc1_b"]),
        "fc2_wt": g["fc2_w"].T, "fc2_b": g["fc2_b"].reshape(1, D),
        "ident_in": np.eye(P, dtype=np.float32),
    }
    arrays = {k: np.ascontiguousarray(v) for k, v in arrays.items()}
    aps = {k: nc.dram_tensor("in_" + k, v.shape, mybir.dt.from_np(v.dtype), kind="ExternalInput").ap()
           for k, v in arrays.items()}
    out = nc.dram_tensor("out", (NB, P, TB, D), F32, kind="ExternalOutput").ap()
    gat_layer(nc, out=out, **aps)
    r = run_bass_kernel_spmd(nc, [{"in_" + k: v for k, v in arrays.items()}], core_ids=[0])
    return r.results[0]["out"].transpose(0, 2, 1, 3).reshape(N, D)
```
